# Optimizing a Trainium2 kernel written in Bass

```python
import numpy as np
import jax
import jax.numpy as jnp

def _softmax(x, axis=-1):
    return jax.nn.softmax(x, axis=axis)

def _gelu(x):
    return jax.nn.gelu(x, approximate=True)

def _silu(x):
    return jax.nn.silu(x)

def _sigmoid(x):
    return jax.nn.sigmoid(x)

def _layernorm(x, axis=-1, eps=1e-05):
    m = jnp.mean(x, axis=axis, keepdims=True)
    v = jnp.var(x, axis=axis, keepdims=True)
    return (x - m) / jnp.sqrt(v + eps)

def _scatter_add(tgt, idx, src, axis=0):
    return tgt.at[idx].add(src)

def _segment_sum(src, seg, n):
    return jax.ops.segment_sum(src, seg, n)
kernel_name = 'mk_cond_resid_d4_seqx_r4_e9d981'

def setup_inputs(seed: int=0):
    np.random.seed(seed)
    _w = jnp.asarray

    def _rec_inputs():
        import jax
        import jax.numpy as jnp
        _rk = jax.random.key(seed)
        x = -0.000125 + 0.9999 * jax.random.normal(jax.random.fold_in(_rk, 1), (8, 256, 512), jnp.float32)
        _lenS = 256 - jax.random.randint(jax.random.fold_in(_rk, 7), (8,), 0, max(1, 256 // 4) + 1, jnp.int32)
        _lenS2 = 256 - jax.random.randint(jax.random.fold_in(_rk, 8), (8,), 0, max(1, 256 // 4) + 1, jnp.int32)
        cond_2048 = 0.000782532 + 0.100527 * jax.random.normal(jax.random.fold_in(_rk, 11), (8, 512), jnp.float32)
        return (x, cond_2048)
    x, cond_2048 = _rec_inputs()

    def _L0_cond_setup():
        import jax, jax.numpy as jnp
        import numpy as np
        key = jax.random.key(seed)
        k1, k2, k3 = jax.random.split(key, 3)
        B, L, D, K = (4, 1024, 512, 4)
        x = jax.random.normal(k1, (B, L, D), dtype=jnp.float32)
        w = jax.random.normal(k2, (K, 1, D), dtype=jnp.float32) * 0.1
        b = jax.random.normal(k3, (D,), dtype=jnp.float32) * 0.1
        return {'x': x, 'w': w, 'b': b}
    _L0_cond_all = _L0_cond_setup()
    _L0_cond_in = {k: v for k, v in _L0_cond_all.items() if k in ('b',)}
    del _L0_cond_all

    def _L1_cond_setup():
        import jax, jax.numpy as jnp
        import numpy as np
        DT = 0.01
        EPSILON = 0.08
        ALPHA = 0.7
        BETA = 0.8
        CLAMP = 20.0
        B, T, N = (64, 128, 512)

        def _derivative(q, p, drive, coupling, bias):
            i_couple = jnp.tanh(q) @ coupling.T
            dq = q - q ** 3 / 3.0 - p + drive + i_couple + bias
            dp = EPSILON * (q + ALPHA - BETA * p)
            return (dq, dp)

        def _rk4_step(q, p, drive, coupling, bias):
            dq1, dp1 = _derivative(q, p, drive, coupling, bias)
            dq2, dp2 = _derivative(q + 0.5 * DT * dq1, p + 0.5 * DT * dp1, drive, coupling, bias)
            dq3, dp3 = _derivative(q + 0.5 * DT * dq2, p + 0.5 * DT * dp2, drive, coupling, bias)
            dq4, dp4 = _derivative(q + DT * dq3, p + DT * dp3, drive, coupling, bias)
            q_next = q + DT / 6.0 * (dq1 + 2 * dq2 + 2 * dq3 + dq4)
            p_next = p + DT / 6.0 * (dp1 + 2 * dp2 + 2 * dp3 + dp4)
            q_next = jnp.clip(q_next, -CLAMP, CLAMP)
            p_next = jnp.clip(p_next, -CLAMP, CLAMP)
            return (q_next, p_next)
        key = jax.random.key(seed)
        k1, k2, k3, k4 = jax.random.split(key, 4)
        return {'q0': jax.random.normal(k1, (B, N), dtype=jnp.float32), 'p0': jax.random.normal(k2, (B, N), dtype=jnp.float32), 'input_drive_seq': jax.random.normal(k3, (B, T, N), dtype=jnp.float32), 'coupling': jax.random.normal(k4, (N, N), dtype=jnp.float32) * 0.01, 'bias': jnp.zeros((N,), dtype=jnp.float32)}
    _L1_cond_all = _L1_cond_setup()
    _L1_cond_in = {k: v for k, v in _L1_cond_all.items() if k in ('coupling', 'bias')}
    del _L1_cond_all

    def _L2_cond_setup():
        import math
        import jax, jax.numpy as jnp
        import numpy as np
        ENCODER_SIZE = 256
        NUM_HEADER = 16
        DK = ENCODER_SIZE // NUM_HEADER
        B, S = (4, 512)
        key = jax.random.key(seed)
        kx, km, kq, kk, kv, ko = jax.random.split(key, 6)
        x = jax.random.normal(kx, (B, ENCODER_SIZE, S), dtype=jnp.float32)
        mask = (jax.random.uniform(km, (B, S)) < 0.9).astype(jnp.float32)
        lim = math.sqrt(6.0 / (ENCODER_SIZE + DK))
        Wq = jax.random.uniform(kq, (NUM_HEADER, ENCODER_SIZE, DK), minval=-lim, maxval=lim, dtype=jnp.float32)
        Wk = jax.random.uniform(kk, (NUM_HEADER, ENCODER_SIZE, DK), minval=-lim, maxval=lim, dtype=jnp.float32)
        Wv = jax.random.uniform(kv, (NUM_HEADER, ENCODER_SIZE, DK), minval=-lim, maxval=lim, dtype=jnp.float32)
        limo = math.sqrt(6.0 / ENCODER_SIZE)
        Wo = jax.random.uniform(ko, (ENCODER_SIZE, ENCODER_SIZE), minval=-limo, maxval=limo, dtype=jnp.float32)
        return {'x': x, 'mask': mask, 'Wq': Wq, 'Wk': Wk, 'Wv': Wv, 'Wo': Wo}
    _L2_cond_all = _L2_cond_setup()
    _L2_cond_in = {k: v for k, v in _L2_cond_all.items() if k in ('Wq', 'Wk', 'Wv', 'Wo')}
    del _L2_cond_all

    def _L3_cond_setup():
        import jax, jax.numpy as jnp
        import numpy as np
        HEADS = 16
        EPS = 1e-06

        def _rms_norm(x, g):
            xf = x.astype(jnp.float32)
            y = xf * jax.lax.rsqrt(jnp.mean(xf * xf, axis=-1, keepdims=True) + EPS)
            return y.astype(x.dtype) * g
        key = jax.random.key(seed)
        ks = jax.random.split(key, 6)
        b, n, dim, emb_dim = (4, 512, 512, 512)
        d_head = dim // HEADS
        return {'x': jax.random.normal(ks[0], (b, n, dim), jnp.float32), 'emb': jax.random.normal(ks[1], (b, 1, emb_dim), jnp.float32), 'W_emb': jax.random.normal(ks[2], (emb_dim, 2 * dim), jnp.float32) * emb_dim ** (-0.5), 'b_emb': jnp.zeros((2 * dim,), jnp.float32), 'g_norm': jnp.ones((dim,), jnp.float32), 'W_qkv': jax.random.normal(ks[3], (dim, 3 * dim), jnp.float32) * dim ** (-0.5), 'g_q': jnp.ones((d_head,), jnp.float32), 'g_k': jnp.ones((d_head,), jnp.float32), 'W_out': jax.random.normal(ks[4], (dim, dim), jnp.float32) * dim ** (-0.5)}
    _L3_cond_all = _L3_cond_setup()
    _L3_cond_in = {k: v for k, v in _L3_cond_all.items() if k in ('W_emb', 'b_emb', 'g_norm', 'W_qkv', 'g_q', 'g_k', 'W_out')}
    del _L3_cond_all
    return {'x': x, 'cond_2048': cond_2048, 'L0_cond_b': _L0_cond_in['b'], 'L1_cond_coupling': _L1_cond_in['coupling'], 'L1_cond_bias': _L1_cond_in['bias'], 'L2_cond_Wq': _L2_cond_in['Wq'], 'L2_cond_Wk': _L2_cond_in['Wk'], 'L2_cond_Wv': _L2_cond_in['Wv'], 'L2_cond_Wo': _L2_cond_in['Wo'], 'L3_cond_W_emb': _L3_cond_in['W_emb'], 'L3_cond_b_emb': _L3_cond_in['b_emb'], 'L3_cond_g_norm': _L3_cond_in['g_norm'], 'L3_cond_W_qkv': _L3_cond_in['W_qkv'], 'L3_cond_g_q': _L3_cond_in['g_q'], 'L3_cond_g_k': _L3_cond_in['g_k'], 'L3_cond_W_out': _L3_cond_in['W_out']}

def reference(x, cond_2048, L0_cond_b, L1_cond_coupling, L1_cond_bias, L2_cond_Wq, L2_cond_Wk, L2_cond_Wv, L2_cond_Wo, L3_cond_W_emb, L3_cond_b_emb, L3_cond_g_norm, L3_cond_W_qkv, L3_cond_g_q, L3_cond_g_k, L3_cond_W_out):
    import jax
    import jax.numpy as jnp

    def _L0_cond_ref(x, w, b):
        import jax, jax.numpy as jnp
        import numpy as np
        'Depthwise causal conv1d, channel-last.\n            x: (B, L, D); w: (K, 1, D); b: (D,). Returns (B, L, D).\n            Matches torch: Conv1d(D, D, K, groups=D, padding=K-1)(x.T)[..., :L].T\n            which is exactly a causal conv (left pad K-1, trim to L).\n            '
        K = w.shape[0]
        D = x.shape[-1]
        y = jax.lax.conv_general_dilated(x, w, window_strides=(1,), padding=[(K - 1, 0)], feature_group_count=D, dimension_numbers=('NWC', 'WIO', 'NWC'))
        return y + b

    def _L1_cond_ref(q0, p0, input_drive_seq, coupling, bias):
        import jax, jax.numpy as jnp
        import numpy as np
        DT = 0.01
        EPSILON = 0.08
        ALPHA = 0.7
        BETA = 0.8
        CLAMP = 20.0
        B, T, N = (64, 128, 512)

        def _derivative(q, p, drive, coupling, bias):
            i_couple = jnp.tanh(q) @ coupling.T
            dq = q - q ** 3 / 3.0 - p + drive + i_couple + bias
            dp = EPSILON * (q + ALPHA - BETA * p)
            return (dq, dp)

        def _rk4_step(q, p, drive, coupling, bias):
            dq1, dp1 = _derivative(q, p, drive, coupling, bias)
            dq2, dp2 = _derivative(q + 0.5 * DT * dq1, p + 0.5 * DT * dp1, drive, coupling, bias)
            dq3, dp3 = _derivative(q + 0.5 * DT * dq2, p + 0.5 * DT * dp2, drive, coupling, bias)
            dq4, dp4 = _derivative(q + DT * dq3, p + DT * dp3, drive, coupling, bias)
            q_next = q + DT / 6.0 * (dq1 + 2 * dq2 + 2 * dq3 + dq4)
            p_next = p + DT / 6.0 * (dp1 + 2 * dp2 + 2 * dp3 + dp4)
            q_next = jnp.clip(q_next, -CLAMP, CLAMP)
            p_next = jnp.clip(p_next, -CLAMP, CLAMP)
            return (q_next, p_next)
        drive_tbn = jnp.swapaxes(input_drive_seq, 0, 1)

        def scan_fn(carry, drive):
            q, p = carry
            q, p = _rk4_step(q, p, drive, coupling, bias)
            return ((q, p), q)
        (_, _), q_trace_tbn = jax.lax.scan(scan_fn, (q0, p0), drive_tbn)
        return jnp.swapaxes(q_trace_tbn, 0, 1)

    def _L2_cond_ref(x, mask, Wq, Wk, Wv, Wo):
        import math
        import jax, jax.numpy as jnp
        import numpy as np
        ENCODER_SIZE = 256
        NUM_HEADER = 16
        DK = ENCODER_SIZE // NUM_HEADER
        B, S = (4, 512)
        num_header = Wq.shape[0]
        dk = Wq.shape[2]
        sqrt_dk_inv = 1.0 / math.sqrt(dk)
        xt = jnp.transpose(x, (0, 2, 1))
        q = xt @ Wq[1]
        k = xt @ Wk[1]
        v = xt @ Wv[1]
        scores = jnp.einsum('bqd,bkd->bqk', q, k) * sqrt_dk_inv
        hmask = mask[:, None, :]
        vmask = mask[:, :, None]
        scores = scores * hmask + (1.0 - hmask) * -1e+30
        attn = jax.nn.softmax(scores, axis=2) * vmask
        head = attn @ v
        heads = jnp.tile(head, (1, 1, num_header))
        out = heads @ Wo
        return jnp.transpose(out, (0, 2, 1))

    def _L3_cond_ref(x, emb, W_emb, b_emb, g_norm, W_qkv, g_q, g_k, W_out):
        import jax, jax.numpy as jnp
        import numpy as np
        HEADS = 16
        EPS = 1e-06

        def _rms_norm(x, g):
            xf = x.astype(jnp.float32)
            y = xf * jax.lax.rsqrt(jnp.mean(xf * xf, axis=-1, keepdims=True) + EPS)
            return y.astype(x.dtype) * g
        b, n, dim = x.shape
        h = HEADS
        d = dim // h
        scale_shift = emb @ W_emb + b_emb
        scale, shift = jnp.split(scale_shift, 2, axis=-1)
        xn = _rms_norm(x, g_norm) * (1.0 + scale) + shift
        qkv = xn @ W_qkv
        qkv = qkv.reshape(b, n, 3, h, d)
        q, k, v = jnp.moveaxis(qkv, 2, 0)
        q = jnp.swapaxes(q, 1, 2)
        k = jnp.swapaxes(k, 1, 2)
        v = jnp.swapaxes(v, 1, 2)
        q = _rms_norm(q, g_q)
        k = _rms_norm(k, g_k)
        logits = jnp.einsum('bhqd,bhkd->bhqk', q, k) * d ** (-0.5)
        attn = jax.nn.softmax(logits, axis=-1)
        o = jnp.einsum('bhqk,bhkd->bhqd', attn, v)
        o = jnp.swapaxes(o, 1, 2).reshape(b, n, dim)
        return o + o @ W_out
    x = x + _L0_cond_ref(x, cond_2048[:, None, :], L0_cond_b)
    x = x + _L1_cond_ref(cond_2048, cond_2048, x, L1_cond_coupling, L1_cond_bias)
    x = x + _L2_cond_ref(x, cond_2048, L2_cond_Wq, L2_cond_Wk, L2_cond_Wv, L2_cond_Wo)
    x = x + _L3_cond_ref(x, cond_2048[:, None, :], L3_cond_W_emb, L3_cond_b_emb, L3_cond_g_norm, L3_cond_W_qkv, L3_cond_g_q, L3_cond_g_k, L3_cond_W_out)
    return x

_drawn_inputs = setup_inputs


def setup_inputs(seed=0):
    import zlib

    import numpy as np

    out = dict(_drawn_inputs(seed))
    spreads = {'L1_cond_bias': (0.0, 0.1),
     'L3_cond_b_emb': (0.0, 0.1),
     'L3_cond_g_norm': (1.0, 0.2),
     'L3_cond_g_q': (1.0, 0.6),
     'L3_cond_g_k': (1.0, 0.6)}
    factors = {}
    for name, (base, spread) in spreads.items():
        noise = np.random.default_rng([zlib.crc32(name.encode()), seed]).standard_normal(out[name].shape)
        drawn = base * np.exp(spread * noise) if base else spread * noise
        out[name] = jnp.asarray(drawn.astype(out[name].dtype))
    for name, factor in factors.items():
        out[name] = (out[name] * factor).astype(out[name].dtype)
    return out
```

```python
from contextlib import ExitStack

import concourse.bass as bass
from concourse import mybir

F32 = mybir.dt.float32
F16 = mybir.dt.float16
I32 = mybir.dt.int32
ALU = mybir.AluOpType
ACT = mybir.ActivationFunctionType
AX = mybir.AxisListType
RMAX = bass.bass_isa.ReduceOp.max

P = 128
DT = 0.01
H = DT / 2
EPSILON, ALPHA, BETA, CLAMP = 0.08, 0.7, 0.8, 20.0
SHIFT = ALPHA / BETA
RMS_EPS = 1e-6
BIG = 3.0e38


class Signal:

    def __init__(self, sem, per, base=0):
        self.sem, self.per, self.base, self.n = sem, per, base, 0

    def by(self, ins):
        self.n += 1
        ins.then_inc(self.sem, 1)
        return self.n

    def wait(self, eng, turn, n):
        eng.wait_ge(self.sem, turn * self.per + (self.base + n))

    def closed(self):
        assert self.n == self.per, (self.n, self.per)


def build(nc, x, cond, L0_b, coupling, L1_bias, Wq, Wk, Wv, Wo, W_emb, b_emb, g_norm, W_qkv, g_q, g_k,
          W_out, out):
    B, T, D = x.shape
    TAPS = cond.shape[0]
    C = D // P
    TC = T // P
    CB = C * B
    HEADS, DK = Wq.shape[0], Wq.shape[2]
    DH = g_q.shape[0]
    NH = D // DH
    HPC = P // DH
    SCALE2 = float(DK) ** -0.5
    SCALE3 = float(DH) ** -0.5
    assert (B, C, TC, TAPS, DK, DH) == (8, 4, 2, 8, 16, 32)

    with ExitStack() as ctx:
        def sb(name, shape, dt=F32):
            return ctx.enter_context(nc.sbuf_tensor(name, shape, dt))

        def sem(name):
            return ctx.enter_context(nc.semaphore(name))

        padded = sb("padded_x", [P, (T + TAPS - 1) * CB])
        drive = sb("drive", [P, T, CB])
        trace = sb("trace", [P, (T + 1) * CB])
        c_hi = sb("c_hi", [P, C, D], F16)
        c_lo = sb("c_lo", [P, C, D], F16)
        wqkv = sb("wqkv", [P, C, 3 * D])
        wout = sb("wout", [P, C, D])
        ident = sb("ident", [P, P])
        coup = trace[:, 0:C * D].rearrange("p (c m) -> p c m", c=C)
        coup_t = trace[:, C * D:2 * C * D].rearrange("p (c n) -> p c n", c=C)
        wemb = trace[:, 2 * C * D:4 * C * D].rearrange("p (c n) -> p c n", c=C)
        tiles = padded[:, 0:8 * TC * D].rearrange("p (i t d) -> p i t d", i=8, t=TC)
        x2t = tiles[:, 0].rearrange("p t d -> p (t d)").rearrange("p (c t) -> p c t", c=C)
        x2, x3, x3n, o_sb, res, x1t = (tiles[:, i] for i in range(1, 7))
        x1t = x1t.rearrange("p t d -> p (t d)").rearrange("p (c t) -> p c t", c=C)
        o_t = tiles[:, 7].rearrange("p t d -> p (t d)").rearrange("p (c t) -> p c t", c=C)

        rows = sb("rows", [16, D])
        cols = sb("cols", [P, C, 16])
        taps = sb("taps", [P, TAPS, CB])
        conv_bias = sb("conv_bias", [P, CB])
        h_sigma = sb("h_sigma", [P, CB])
        neg_bias = sb("neg_bias", [P, C])
        cmax = sb("cmax", [P, 2])
        cmaxb = sb("bias_sum", [P, C])
        ebits = sb("ebits", [P, 2], I32)
        pow2 = sb("pow2", [P, 2])
        cs = sb("consts", [P, 10])
        bounds = sb("bounds", [P, 4])
        gains = sb("gains", [P, 2])
        Z = [sb(f"stage{k}_qp", [P, 2 * CB]) for k in range(4)]
        tanh_hl = sb("tanh_hl", [P, C, 2 * B], F16)
        tanh_f = sb("tanh_f", [P, CB])
        qsq = sb("qsq", [P, CB])
        yv = sb("q_minus_beta_p", [P, CB])
        wv_ = sb("linear_part", [P, CB])
        cub = sb("cubic_part", [P, CB])
        q_hd = sb("q_plus_drive", [P, CB])
        q_hd2 = sb("half_q_plus_drive", [P, CB])
        acc_hd = sb("acc_plus_drive", [P, CB])
        acc = sb("acc_qp", [P, 2 * CB])
        q3 = sb("q3_sum", [P, CB])
        qv = sb("q_unclipped", [P, CB])
        p3 = sb("p3_sum", [P, CB])
        q4h = sb("stage3_half_q", [P, CB])
        prod = sb("prod", [P, TAPS * CB])
        half = sb("half_sum", [P, 4 * CB])
        quart = sb("quarter_sum", [P, 2 * CB])
        conv = sb("conv", [P, CB])
        xb = sb("x_plus_bias", [P, CB])
        dsum = sb("dsum", [P, CB])
        wqk2 = sb("wqk2", [P, TC, P])
        wv2 = sb("wv2", [P, TC, DK])
        wo2 = sb("wo2", [P, 2, T])
        fold = sb("fold", [P, DK])
        wo_sum = sb("wo_sum", [DK, T])
        params = sb("params", [P, B, 12])
        par = sb("par", [P, 12])
        hmask = sb("hmask", [DK, D])
        q2t = sb("q2t", [P, D])
        k2t = sb("k2t", [P, D])
        v2 = sb("v2", [P, C, DK + 1])
        negmax2 = sb("negmax2", [P, C])
        e2 = sb("e2", [P, C, D])
        rden2 = sb("rden2", [P, C])
        rmask2 = sb("rmask2", [P, C])
        head2 = sb("head2", [P, C, DK])
        head2t = sb("head2t", [DK, D])
        ss3 = sb("ss3", [P, TC])
        ms3 = sb("ms3", [P, TC])
        r3 = sb("r3", [P, TC])
        xnt = sb("xnt", [P, C, T])
        sqs = [sb(f"sq_{i}", [P, D]) for i in range(2)]
        hss = sb("head_ss", [P, 4, NH])
        hms = sb("head_ms", [P, 4, NH])
        hr = sb("head_r", [P, 4, NH])
        halves = sb("minus_half", [P, NH])
        qkn = [sb(f"qkn_{i}", [P, D]) for i in range(2)]
        qt = sb("qt", [P, C, T])
        kt = sb("kt", [P, C, T])
        v3 = sb("v3", [P, TC, D])
        negmax3 = sb("negmax3", [P, 2, TC])
        e3 = [sb(f"e3_{i}", [P, TC, T]) for i in range(2)]
        e3t = [sb(f"e3t_{i}", [P, TC, T]) for i in range(2)]
        den3 = sb("den3", [P, TC, NH])
        rden3 = sb("rden3", [P, TC, NH])
        xl = [e2[:, j] for j in range(4)]

        bank = [ctx.enter_context(nc.psum_tensor(f"bank{i}", [P, 512], F32)) for i in range(5)]
        psC = ctx.enter_context(nc.psum_tensor("psC", [P, 4, 256], F32))
        bank += [psC[:, 0:2, :].rearrange("p a b -> p (a b)"), psC[:, 2:4, :].rearrange("p a b -> p (a b)")]
        bank.append(ctx.enter_context(nc.psum_tensor("bank7", [P, 512], F32)))
        psS = psC[:, 0:3, 0:CB]

        s_ld = sem("weights_loaded")
        s_lc = sem("coupling_loaded")
        s_lr = sem("rows_loaded")
        s_rowz = sem("rows_cleared")
        s_id = sem("identity_ready")
        s_pool = sem("pool_chain")
        s_colp = sem("cols_transposed")
        s_cols = sem("cols_ready")
        s_cm = sem("coupling_max")
        s_cma = sem("coupling_max_all")
        s_ct = sem("coupling_transposed")
        s_cte = sem("coupling_evacuated")
        s_vec0 = sem("vector_chain_prep")
        s_par = sem("conv_params_ready")
        s_const = sem("consts_ready")
        s_chi = sem("c_hi_ready")
        s_emb = sem("emb_products")
        s_prm = sem("params_ready")
        s_fold = sem("fold_ready")
        s_wos = sem("wo_products")
        s_xl = [sem(f"x_loaded{j}") for j in range(4)]
        s_xt = sem("x_transposed")
        s_xe = [sem(f"x_evacuated{j}") for j in range(2)]
        s_pad = sem("pad_cleared")
        s_drv = sem("drive_ready")
        s_q = [sem(f"stage{k}_q_ready") for k in range(4)]
        s_hi = [sem(f"stage{k}_tanh_hi") for k in range(4)]
        s_tf = [sem(f"stage{k}_tanh_f") for k in range(4)]
        s_sq = [sem(f"stage{k}_q_squared") for k in range(4)]
        s_lo = [sem(f"stage{k}_tanh_lo") for k in range(4)]
        s_mm = [sem(f"stage{k}_coupling") for k in range(4)]
        s_z4 = sem("stage3_q_scaled")
        s_qv = sem("q_bounded_above")
        s_clip = sem("q_clipped")
        s_p0 = sem("stage0_p")
        s_p = [None] + [sem(f"stage{k}_p") for k in range(1, 4)]
        s_y = [sem(f"stage{k}_y") for k in range(4)]
        s_acc = sem("stage3_acc")
        s_hd = [sem("stage0_q_plus_drive"), None, None, sem("stage3_acc_plus_drive")]
        s_w = [sem(f"stage{k}_linear") for k in range(4)]
        s_b = [sem(f"stage{k}_addend") for k in range(4)]
        s_tr = sem("trace_done")

        block = ctx.enter_context(nc.Block())

        def r8(a):
            return a.rearrange("p (c b) -> p c b", b=B)

        def signal(name, per):
            return Signal(sem(name), per, 1)

        def tail_signals():
            return dict(
                hm=signal("hmask_loaded", 32), hm_done=signal("mask_row_ready", 2),
                par=signal("batch_params", 1),
                x2t=signal("x2t_ready", 5), xtr=signal("x2_transposed", 2), x2=signal("x2_ready", 2),
                proj=signal("l2_proj", 2), qkv2=signal("l2_qkv_ready", 2),
                kk=signal("l2_keys_ready", 1), sc=signal("l2_scores", 4), mx=signal("l2_max", 4), mt=signal("l2_max_row", 1),
                mrow=signal("l2_max_ready", 1), st=signal("l2_scores_t", 4), e2=signal("l2_exp", 4),
                pv=signal("l2_pv", 1), h2=signal("l2_head", 3), h2t=signal("l2_head_t", 1),
                h2e=signal("l2_head_t_ready", 1), o2=signal("l2_out", 2), x3=signal("x3_ready", 2),
                ss=signal("x3_squares", 2), ms=signal("x3_mean", 1), r3=signal("x3_rms", 1),
                x3n=signal("x3_normed", 2), xnp=signal("xn_transposed", 2), xnt=signal("xnt_ready", 4),
                qkv=signal("l3_qkv", 6), sqr=signal("qk_squares", 4), hs=signal("qk_sums", 4),
                hm3=signal("qk_means", 4), hr=signal("qk_rms", 4), qkn=signal("qk_normed", 4),
                v3=signal("v3_ready", 2), qkp=signal("qk_transposed", 4), qkt=signal("qkt_ready", 4),
                s3=signal("l3_scores", NH), m3=signal("l3_max", NH), e3=signal("l3_exp", NH),
                et=signal("l3_probs_t", NH), ete=signal("l3_probs_t_ready", NH), pv3=signal("l3_pv", NH),
                rd=signal("l3_rden", 1), on=signal("l3_o_ready", 2), ot=signal("l3_o_t", 2),
                ote=signal("l3_o_t_ready", 2), op=signal("l3_out", 2), rs=signal("res_part", 2),
                res=signal("res_ready", 2), stored=signal("stored", 32))

        S = tail_signals()

        @block.sync
        def _(sp):
            for signal_ in (s_xt, *s_xe, *(one_.sem for one_ in S.values())):
                sp.sem_inc(signal_, 1)
            sp.dma_start(coup, coupling.rearrange("(c p) m -> p c m", p=P)).then_inc(s_lc, 16)
            one = lambda a: a.rearrange("(o d) -> o d", o=1)
            sp.dma_start(rows[0:B, :], cond).then_inc(s_lr, 16)
            for r, v in ((8, one(L0_b)), (9, one(L1_bias)), (10, one(g_norm)), (11, one(b_emb[0:D])),
                         (12, one(b_emb[D:2 * D])), (15, one(L0_b))):
                sp.dma_start(rows[r:r + 1, :], v).then_inc(s_lr, 16)
            for r, v in ((13, g_q), (14, g_k)):
                sp.dma_start(rows[r:r + 1, :].rearrange("o (h d) -> o h d", d=DH),
                             one(v).unsqueeze(1).to_broadcast([1, NH, DH])).then_inc(s_lr, 16)
            with sp.Fori(0, B // 2) as i:
                for j in range(4):
                    sp.wait_ge(s_xt, i * 4 + 1)
                    sp.dma_start(xl[j], x[bass.ds(i * 2 + j // 2, 1), (j % 2) * P:(j % 2 + 1) * P, :]
                                 .rearrange("o t d -> (o t) d")).then_inc(s_xl[j], 16)
            sp.dma_start(wemb, W_emb.rearrange("(c p) n -> p c n", p=P)).then_inc(s_ld, 16)
            sp.wait_ge(s_rowz, 1)
            sp.dma_start(wqk2[:, :, 0:DK], Wq[1].rearrange("(c p) k -> p c k", p=P)).then_inc(s_ld, 16)
            sp.dma_start(wqk2[:, :, 32:32 + DK], Wk[1].rearrange("(c p) k -> p c k", p=P)).then_inc(s_ld, 16)
            sp.dma_start(wv2[:], Wv[1].rearrange("(c p) k -> p c k", p=P)).then_inc(s_ld, 16)
            sp.dma_start(wo2[:], Wo.rearrange("(c p) t -> p c t", p=P)).then_inc(s_ld, 16)
            sp.dma_start(wqkv[:], W_qkv.rearrange("(c p) n -> p c n", p=P)).then_inc(s_ld, 16)
            sp.dma_start(wout[:], W_out.rearrange("(c p) n -> p c n", p=P)).then_inc(s_ld, 16)
            with sp.Fori(0, B) as b:
                S["st"].wait(sp, b, 0)
                row = cond[bass.ds(b, 1), :]
                sp.dma_start(hmask[:], row.to_broadcast([DK, D])).then_inc(S["hm"].sem, 16)
                sp.dma_start(k2t[32:33, :], row).then_inc(S["hm"].sem, 16)
                for tc in range(TC):
                    S["res"].wait(sp, b, tc + 1)
                    sp.dma_start(out[bass.ds(b, 1), tc * P:(tc + 1) * P, :].rearrange("o t d -> (o t) d"),
                                 res[:, tc]).then_inc(S["stored"].sem, 16)
            sp.wait_ge(S["stored"].sem, 32 * B + 1)

        @block.gpsimd
        def _(pool):
            g = nc.gpsimd
            g.memset(ident[:], 0.0).then_inc(s_pool, 1)
            pool.wait_ge(s_pool, 1)
            g.affine_select(out=ident[:], in_=ident[:], compare_op=ALU.not_equal, fill=1.0, base=0,
                            pattern=[[-1, P]], channel_multiplier=1).then_inc(s_id, 1)
            g.memset(wqk2[:], 0.0).then_inc(s_rowz, 1)
            g.memset(padded[:, 0:(TAPS - 1) * CB], 0.0).then_inc(s_pad, 1)
            g.memset(halves[:], -0.5)
            g.memset(q2t[:], 0.0)
            g.memset(k2t[:], 0.0)
            g.memset(v2[:], 1.0).then_inc(s_pool, 1)
            pool.wait_ge(s_pool, 2)
            g.memset(q2t[32:33, :], 1.0)
            g.memset(k2t[64:65, :], 1.0).then_inc(s_pool, 1)
            pool.wait_ge(s_pool, 3)
            pool.wait_ge(s_cm, 1)
            g.partition_all_reduce(cmax[:, 1:2], cmax[:, 0:1], P, RMAX).then_inc(s_cma, 1)
            pool.wait_ge(s_par, 1)
            pool.wait_ge(s_pool, 3)
            pool.wait_ge(s_pad, 1)
            for e in s_xe:
                pool.wait_ge(e, B + 1)
            ch = Signal(s_pool, 6, 3)
            with pool.Fori(0, T) as t:
                ch.wait(pool, t, 0)
                win = padded[:, bass.ds(t * CB, TAPS * CB)]
                g.tensor_tensor(prod[:], win, taps[:].rearrange("p k c -> p (k c)"), ALU.mult).then_inc(s_pool, 1)
                g.tensor_tensor(xb[:], padded[:, bass.ds(t * CB + (TAPS - 1) * CB, CB)], conv_bias[:],
                                ALU.add).then_inc(s_pool, 1)
                ch.wait(pool, t, 2)
                g.tensor_tensor(half[:], prod[:, 0:4 * CB], prod[:, 4 * CB:8 * CB], ALU.add).then_inc(s_pool, 1)
                ch.wait(pool, t, 3)
                g.tensor_tensor(quart[:], half[:, 0:2 * CB], half[:, 2 * CB:4 * CB], ALU.add).then_inc(s_pool, 1)
                ch.wait(pool, t, 4)
                g.tensor_tensor(conv[:], quart[:, 0:CB], quart[:, CB:2 * CB], ALU.add).then_inc(s_pool, 1)
                ch.wait(pool, t, 5)
                g.tensor_tensor(dsum[:], conv[:], xb[:], ALU.add).then_inc(s_pool, 1)
                ch.wait(pool, t, 6)
                g.tensor_tensor(drive[:, bass.ds(t, 1), :].rearrange("p o c -> p (o c)"), dsum[:], h_sigma[:],
                                ALU.mult).then_inc(s_drv, 1)
            pool.wait_ge(s_prm, 1)
            with pool.Fori(0, B) as b:
                S["xnt"].wait(pool, b, 0)
                S["h2"].wait(pool, b, 0)
                S["par"].by(g.tensor_copy(par[:], params[:, bass.ds(b, 1), :].rearrange("p o c -> p (o c)")))
                S["ms"].wait(pool, b, 1)
                S["r3"].by(g.tensor_tensor(r3[:], ms3[:], halves[:, 0:TC], ALU.pow))
                for i in range(4):
                    S["hm3"].wait(pool, b, i + 1)
                    S["hr"].by(g.tensor_tensor(hr[:, i], hms[:, i], halves[:], ALU.pow))

        @block.scalar
        def _(act):
            a = nc.scalar
            with act.Fori(0, B // 2) as i:
                for j in (1, 3):
                    act.wait_ge(s_xt, i * 4 + (j + 2))
                    bb, tc = i * 2 + j // 2, j % 2
                    dst = padded[:, (TAPS - 1 + tc * P) * CB:(TAPS - 1 + (tc + 1) * P) * CB] \
                        .rearrange("p (t c b) -> p b c t", c=C, b=B)
                    a.copy(dst[:, bass.ds(bb, 1)].rearrange("p o c t -> p (o c) t"),
                           bank[j][:].rearrange("p (c t) -> p c t", c=C)).then_inc(s_xe[1], 1)
            a.preload_act_table(ACT.Tanh)
            act.wait_ge(s_const, 1)
            scale = []
            for j in range(3):
                reg = act.alloc_register(f"tanh_scale{j}")
                act.reg_load(reg, cs[0:1, j:j + 1].bitcast(I32))
                scale.append(reg)
            with act.Fori(0, T) as t:
                step = act.snap(t + 1)
                for k in range(4):
                    src, s = ((q3[:], scale[2]), (Z[1][:, 0:CB], scale[0]), (Z[2][:, 0:CB], scale[0]),
                              (q4h[:], scale[1]))[k]
                    act.wait_ge(s_q[k], step)
                    a.activation(tanh_hl[:, :, 0:B], r8(src), ACT.Tanh, scale=s).then_inc(s_hi[k], 1)
                    a.activation(tanh_f[:], src, ACT.Tanh, scale=s).then_inc(s_tf[k], 1)
                    if k == 3:
                        a.activation(Z[3][:, 0:CB], src, ACT.Copy, scale=2.0).then_inc(s_z4, 1)
                    if k == 0:
                        act.wait_ge(s_clip, step)
                        a.activation(qsq[:], Z[0][:, 0:CB], ACT.Square, scale=scale[0]).then_inc(s_sq[0], 1)
                        a.activation(trace[:, bass.ds(t * CB, CB)], Z[0][:, 0:CB], ACT.Copy)
                    else:
                        a.activation(qsq[:], src, ACT.Square, scale=s).then_inc(s_sq[k], 1)
            act.wait_ge(s_clip, T + 1)
            a.activation(trace[:, T * CB:(T + 1) * CB], Z[0][:, 0:CB], ACT.Copy).then_inc(s_tr, 1)
            a.preload_act_table(ACT.Exp)
            with act.Fori(0, B) as b:
                S["xtr"].wait(act, b, 1)
                S["o2"].wait(act, b, 0)
                S["x3"].wait(act, b, 0)
                S["x2"].by(a.copy(x2[:, 0], bank[0][:]))
                S["proj"].wait(act, b, 1)
                S["st"].wait(act, b, 0)
                S["qkv2"].by(a.activation(q2t[0:DK, :], bank[2][0:DK, :], ACT.Copy, scale=SCALE2))
                S["proj"].wait(act, b, 2)
                S["pv"].wait(act, b, 0)
                S["qkv2"].by(a.copy(v2[:, :, 0:DK], bank[3][:, 0:C * DK].rearrange("p (c k) -> p c k", c=C)))
                S["mt"].wait(act, b, 1)
                S["mrow"].by(a.copy(q2t[64:65, :], bank[2][0:1, :]))
                for kc in range(C):
                    S["st"].wait(act, b, kc + 1)
                    S["e2"].by(a.activation(e2[:, kc], bank[kc % 2][:], ACT.Exp))
                S["h2t"].wait(act, b, 1)
                S["h2e"].by(a.copy(head2t[:], bank[2][0:DK, :]))
                for tc in range(TC):
                    S["x3"].wait(act, b, tc + 1)
                    S["ss"].by(a.activation(sqs[tc][:], x3[:, tc], ACT.Square, accum_out=ss3[:, tc:tc + 1]))
                S["par"].wait(act, b, 1)
                for dc in range(C):
                    if dc % 2 == 0:
                        S["xnp"].wait(act, b, dc // 2 + 1)
                    S["xnt"].by(a.activation(xnt[:, dc], bank[2 + dc // 2][:, (dc % 2) * T:(dc % 2 + 1) * T],
                                             ACT.Identity, bias=par[:, 8 + dc:9 + dc], scale=par[:, 4 + dc:5 + dc]))
                for tc in range(TC):
                    for j in range(3):
                        m = tc * 3 + j
                        S["qkv"].wait(act, b, m + 1)
                        if j < 2:
                            i = tc * 2 + j
                            if i >= 2:
                                S["hs"].wait(act, b, i - 1)
                            S["sqr"].by(a.activation(sqs[i % 2][:], bank[m][:], ACT.Square))
                        else:
                            S["v3"].by(a.copy(v3[:, tc], bank[m][:]))
                for i in range(4):
                    tc, j = i // 2, i % 2
                    S["qkp"].wait(act, b, i + 1)
                    S["qkt"].by(a.activation((qt, kt)[j][:, :, tc * P:(tc + 1) * P],
                                             bank[6 + i % 2][:].rearrange("p (c t) -> p c t", c=C), ACT.Copy,
                                             scale=gains[:, j:j + 1]))
                for h in range(NH):
                    S["m3"].wait(act, b, h + 1)
                    if h >= 2:
                        S["et"].wait(act, b, h - 1)
                    for tc in range(TC):
                        e = a.activation(e3[h % 2][:, tc], bank[h % 2][:, tc * T:(tc + 1) * T], ACT.Exp,
                                         bias=negmax3[:, h % 2, tc:tc + 1],
                                         accum_out=den3[:, tc, h:h + 1])
                    S["e3"].by(e)
                for tc in range(TC):
                    S["ot"].wait(act, b, tc + 1)
                    S["ote"].by(a.copy(o_t[:, 2 * tc:2 * tc + 2], bank[tc][:].rearrange("p (c t) -> p c t", c=2)))

        @block.tensor
        def _(pe):
            mm = nc.tensor.matmul
            tr = nc.tensor.transpose
            pe.wait_ge(s_id, 1)
            pe.wait_ge(s_lr, 16 * 9)
            for c in range(C):
                ins = tr(bank[4][:, c * 16:(c + 1) * 16], rows[:, c * P:(c + 1) * P], ident[0:16, 0:16])
            ins.then_inc(s_colp, 1)
            with pe.Fori(0, B // 2) as i:
                for j in range(4):
                    pe.wait_ge(s_xl[j], i * 16 + 16)
                    pe.wait_ge(s_xe[j % 2], i * 2 + (j // 2 + 1))
                    for c in range(C):
                        ins = tr(bank[j][:, c * P:(c + 1) * P], xl[j][:, c * P:(c + 1) * P], ident[:])
                    ins.then_inc(s_xt, 1)
            pe.wait_ge(s_lc, 16)
            for mc in range(C):
                pe.wait_ge(s_xe[mc % 2], B + 1)
                for n in range(C):
                    ins = tr(bank[mc][:, n * P:(n + 1) * P], coup[:, n, mc * P:(mc + 1) * P], ident[:])
                ins.then_inc(s_ct, 1)
            pe.wait_ge(s_ld, 16 * 7)
            pe.wait_ge(s_cols, 1)
            for n in range(2 * C):
                for c in range(C):
                    ins = mm(bank[4][:, 64 + n * B:64 + (n + 1) * B], wemb[:, c, n * P:(n + 1) * P], cols[:, c, 0:B],
                             start=(c == 0), stop=(c == C - 1))
            ins.then_inc(s_emb, 1)
            pe.wait_ge(s_fold, 1)
            for c in range(2):
                ins = mm(bank[7][0:DK, 0:T], fold[:], wo2[:, c], start=(c == 0), stop=(c == 1))
            ins.then_inc(s_wos, 1)

            pe.wait_ge(s_chi, 2)
            with pe.Fori(0, T) as t:
                step = pe.snap(t + 1)
                for k in range(4):
                    pe.wait_ge(s_hi[k], step)
                    for kc in range(C):
                        for m in range(C):
                            mm(psC[:, 0, m * B:(m + 1) * B], c_lo[:, kc, m * P:(m + 1) * P], tanh_hl[:, kc, 0:B],
                               start=(kc == 0 and m == 0), stop=False, skip_group_check=True)
                    pe.wait_ge(s_lo[k], step)
                    for m in range(C):
                        for kc in range(C):
                            ins = mm(psC[:, 0:2, m * B:(m + 1) * B], c_hi[:, kc, m * P:(m + 1) * P],
                                     tanh_hl[:, kc, :].rearrange("p (s b) -> p s b", s=2),
                                     start=False, stop=(kc == C - 1 and m == C - 1), skip_group_check=True)
                    ins.then_inc(s_mm[k], 1)
            pe.wait_ge(s_q[0], T + 1)
            with pe.Fori(0, B) as b:
                for tc in range(TC):
                    S["x2t"].wait(pe, b, 5)
                    if tc == 0:
                        S["ote"].wait(pe, b, 0)
                        S["res"].wait(pe, b, 0)
                    for c in range(C):
                        ins = tr(bank[tc][:, c * P:(c + 1) * P], x2t[:, c, tc * P:(tc + 1) * P], ident[:])
                    S["xtr"].by(ins)
                S["x2"].wait(pe, b, 2)
                for tc in range(TC):
                    ins = mm(bank[2][:], wqk2[:, tc], x2[:, tc], start=(tc == 0), stop=(tc == TC - 1))
                S["proj"].by(ins)
                for c in range(C):
                    for tc in range(TC):
                        ins = mm(bank[3][:, c * DK:(c + 1) * DK], x2[:, tc, c * P:(c + 1) * P], wv2[:, tc],
                                 start=(tc == 0), stop=(tc == TC - 1))
                S["proj"].by(ins)
                S["qkv2"].wait(pe, b, 2)
                S["kk"].wait(pe, b, 1)
                S["hm_done"].wait(pe, b, 2)
                for qc in range(C):
                    if qc >= 2:
                        S["mx"].wait(pe, b, qc - 1)
                    S["sc"].by(mm(bank[qc % 2][:], q2t[0:33, qc * P:(qc + 1) * P], k2t[0:33, :], start=True, stop=True))
                S["mx"].wait(pe, b, 4)
                for qc in range(C):
                    ins = tr(bank[2][0:1, qc * P:(qc + 1) * P], negmax2[:, qc:qc + 1], ident[:])
                S["mt"].by(ins)
                S["mrow"].wait(pe, b, 1)
                for kc in range(C):
                    if kc >= 2:
                        S["e2"].wait(pe, b, kc - 1)
                    S["st"].by(mm(bank[kc % 2][:], k2t[0:65, kc * P:(kc + 1) * P], q2t[0:65, :], start=True, stop=True))
                S["e2"].wait(pe, b, 4)
                for qc in range(C):
                    for kc in range(C):
                        ins = mm(bank[3][:, 128 + qc * 17:128 + (qc + 1) * 17], e2[:, kc, qc * P:(qc + 1) * P], v2[:, kc],
                                 start=(kc == 0), stop=(kc == C - 1))
                S["pv"].by(ins)
                S["h2"].wait(pe, b, 3)
                for qc in range(C):
                    ins = tr(bank[2][0:DK, qc * P:(qc + 1) * P], head2[:, qc], ident[:])
                S["h2t"].by(ins)
                S["h2e"].wait(pe, b, 1)
                for tc in range(TC):
                    S["o2"].by(mm(bank[tc][:], wo_sum[:, tc * P:(tc + 1) * P], head2t[:], start=True, stop=True))
                for dc in range(C):
                    for tc in range(TC):
                        S["x3n"].wait(pe, b, tc + 1)
                        ins = tr(bank[2 + dc // 2][:, (dc % 2) * T + tc * P:(dc % 2) * T + (tc + 1) * P],
                                 x3n[:, tc, dc * P:(dc + 1) * P], ident[:])
                    if dc % 2:
                        S["xnp"].by(ins)
                S["xnt"].wait(pe, b, 4)
                for tc in range(TC):
                    for j in range(3):
                        m = tc * 3 + j
                        for dc in range(C):
                            ins = mm(bank[m][:], xnt[:, dc, tc * P:(tc + 1) * P], wqkv[:, dc, j * D:(j + 1) * D],
                                     start=(dc == 0), stop=(dc == C - 1))
                        S["qkv"].by(ins)
                for i in range(4):
                    S["qkn"].wait(pe, b, i + 1)
                    if i >= 2:
                        S["qkt"].wait(pe, b, i - 1)
                    for c in range(C):
                        ins = tr(bank[6 + i % 2][:, c * P:(c + 1) * P], qkn[i % 2][:, c * P:(c + 1) * P], ident[:])
                    S["qkp"].by(ins)
                S["qkt"].wait(pe, b, 4)
                S["v3"].wait(pe, b, 2)

                def scores(h):
                    c, r = h // HPC, (h % HPC) * DH
                    if h >= 2:
                        S["e3"].wait(pe, b, h - 1)
                    for tc in range(TC):
                        ins = mm(bank[h % 2][:, tc * T:(tc + 1) * T], qt[r:r + DH, c, tc * P:(tc + 1) * P],
                                 kt[r:r + DH, c, :], start=True, stop=True)
                    S["s3"].by(ins)

                def turn(h):
                    S["e3"].wait(pe, b, h + 1)
                    if h >= 2:
                        S["ete"].wait(pe, b, h - 1)
                    for kc in range(TC):
                        for tc in range(TC):
                            ins = tr(bank[2 + h % 2][:, kc * T + tc * P:kc * T + (tc + 1) * P],
                                     e3[h % 2][:, tc, kc * P:(kc + 1) * P], ident[:])
                    S["et"].by(ins)

                def pv(h):
                    S["ete"].wait(pe, b, h + 1)
                    for tc in range(TC):
                        for kc in range(TC):
                            ins = mm(bank[4 + tc][:, h * DH:(h + 1) * DH], e3t[h % 2][:, kc, tc * P:(tc + 1) * P],
                                     v3[:, kc, h * DH:(h + 1) * DH], start=(kc == 0), stop=(kc == TC - 1))
                    S["pv3"].by(ins)

                scores(0)
                scores(1)
                for h in range(NH):
                    turn(h)
                    if h + 2 < NH:
                        scores(h + 2)
                    if h >= 1:
                        pv(h - 1)
                pv(NH - 1)
                for dc in range(C):
                    for tc in range(TC):
                        S["on"].wait(pe, b, tc + 1)
                        ins = tr(bank[dc // 2][:, (dc % 2) * T + tc * P:(dc % 2) * T + (tc + 1) * P],
                                 o_sb[:, tc, dc * P:(dc + 1) * P], ident[:])
                    if dc % 2:
                        S["ot"].by(ins)
                S["ote"].wait(pe, b, 2)
                for tc in range(TC):
                    for dc in range(C):
                        ins = mm(bank[6 + tc][:], o_t[:, dc, tc * P:(tc + 1) * P], wout[:, dc], start=(dc == 0),
                                 stop=(dc == C - 1))
                    S["op"].by(ins)

        @block.vector
        def _(dve):
            v = nc.vector
            STT = v.scalar_tensor_tensor
            chain = [0]

            def link(ins):
                chain[0] += 1
                ins.then_inc(s_vec0, 1)
                dve.wait_ge(s_vec0, chain[0])

            dve.wait_ge(s_lc, 16)
            v.tensor_reduce(cmax[:, 0:1], coup.rearrange("p c m -> p (c m)"), AX.X, ALU.max,
                            apply_absolute_value=True).then_inc(s_cm, 1)
            dve.wait_ge(s_colp, 1)
            v.tensor_copy(cols[:].rearrange("p c r -> p (c r)"), bank[4][:, 0:64]).then_inc(s_cols, 1)
            dve.wait_ge(s_cols, 1)
            dve.wait_ge(s_cma, 1)
            link(v.tensor_scalar(pow2[:, 0:1], cmax[:, 1:2], H, 2.0 ** -40, ALU.mult, ALU.max))
            link(v.tensor_scalar(pow2[:, 0:1], pow2[:, 0:1], 2.0 ** 60, None, ALU.min))
            link(v.tensor_scalar(ebits[:, 0:1], pow2[:, 0:1].bitcast(I32), 0x7F800000, None, ALU.bitwise_and))
            link(v.tensor_scalar(ebits[:, 1:2], ebits[:, 0:1], -1.0, float(254 << 23), ALU.mult, ALU.add))
            two_e, two_me = ebits[:, 0:1].bitcast(F32), ebits[:, 1:2].bitcast(F32)
            for n, (src, f) in enumerate(((two_e, 2.0 ** -14), (two_e, 2.0 ** -13), (two_e, 2.0 ** -14 / 3),
                                          (two_me, H * 2.0 ** 14), (two_me, CLAMP * 2.0 ** 14),
                                          (two_me, -CLAMP * 2.0 ** 14), (two_me, (CLAMP - SHIFT) * 2.0 ** 14),
                                          (two_me, (-CLAMP - SHIFT) * 2.0 ** 14), (two_me, -SHIFT * 2.0 ** 14),
                                          (two_e, 2.0 ** -14 / H))):
                v.tensor_scalar(cs[:, n:n + 1], src, f, None, ALU.mult)
            link(v.tensor_scalar(pow2[:, 1:2], two_me, 2.0 ** 14, None, ALU.mult))
            v.tensor_copy(taps[:].rearrange("p k (c b) -> p k c b", b=B),
                          cols[:, :, 0:TAPS].rearrange("p c k -> p k c").unsqueeze(3).to_broadcast([P, TAPS, C, B]))
            link(v.tensor_scalar(neg_bias[:], cols[:, :, 9], -1.0, SHIFT, ALU.mult, ALU.add))
            link(v.tensor_tensor(cmaxb[:], cols[:, :, 8], neg_bias[:], ALU.subtract))
            v.tensor_copy(r8(conv_bias[:]), cmaxb[:].unsqueeze(2).to_broadcast([P, C, B]))
            v.tensor_copy(h_sigma[:], cs[:, 3:4].to_broadcast([P, CB])).then_inc(s_par, 1)
            v.memset(bounds[:, 0:1], BIG)
            v.memset(bounds[:, 1:2], -BIG)
            v.memset(bounds[:, 2:3], BIG)
            link(v.memset(bounds[:, 3:4], -BIG))
            link(v.tensor_scalar(r8(Z[0][:, 0:CB]), cols[:, :, 0:B], pow2[:, 1:2], None, ALU.mult))
            v.tensor_scalar(q3[:], Z[0][:, 0:CB], 3.0, None, ALU.mult)
            link(v.tensor_scalar(p3[:], Z[0][:, 0:CB], cs[:, 8:9], None, ALU.add))
            link(v.tensor_copy(gains[:, 0:1], cols[:, 0, 13:14]))
            link(v.tensor_scalar(gains[:, 1:2], cols[:, 0, 14:15], SCALE3, None, ALU.mult))
            v.tensor_reduce(fold[:], ident[:].rearrange("p (a j) -> p j a", j=DK), AX.X, ALU.add).then_inc(s_fold, 1)
            with dve.Fori(0, B // 2) as i:
                for j in (0, 2):
                    dve.wait_ge(s_xt, i * 4 + (j + 2))
                    bb, tc = i * 2 + j // 2, j % 2
                    dst = padded[:, (TAPS - 1 + tc * P) * CB:(TAPS - 1 + (tc + 1) * P) * CB] \
                        .rearrange("p (t c b) -> p b c t", c=C, b=B)
                    v.tensor_copy(dst[:, bass.ds(bb, 1)].rearrange("p o c t -> p (o c) t"),
                                  bank[j][:].rearrange("p (c t) -> p c t", c=C)).then_inc(s_xe[0], 1)
            for mc in range(C):
                dve.wait_ge(s_ct, mc + 1)
                link(v.tensor_scalar(coup_t[:, mc], bank[mc][:], H, pow2[:, 1:2], ALU.mult, ALU.mult))
                link(v.tensor_copy(c_hi[:, mc], coup_t[:, mc]))
                ins = v.tensor_tensor(c_lo[:, mc], coup_t[:, mc], c_hi[:, mc], ALU.subtract)
            ins.then_inc(s_chi, 1)
            dve.wait_ge(s_emb, 1)
            emb = bank[4][:, 64:64 + 2 * CB].rearrange("p (n b) -> p n b", b=B)
            pr = params[:].rearrange("p b n -> p n b")
            v.tensor_copy(pr[:, 0:4], cols[:, :, 0:B])
            bc = lambda r: cols[:, :, r:r + 1].to_broadcast([P, C, B])
            v.tensor_tensor(pr[:, 8:12], emb[:, 4:8], bc(12), ALU.add)
            link(v.tensor_tensor(pr[:, 4:8], emb[:, 0:4], bc(11), ALU.add))
            link(v.tensor_scalar(pr[:, 4:8], pr[:, 4:8], 1.0, None, ALU.add))
            v.tensor_tensor(pr[:, 4:8], pr[:, 4:8], bc(10), ALU.mult).then_inc(s_prm, 1)
            dve.wait_ge(s_wos, 1)
            link(v.tensor_copy(wo_sum[:], bank[7][0:DK, 0:T]))
            v.tensor_scalar(q3[:], Z[0][:, 0:CB], 3.0, None, ALU.mult).then_inc(s_chi, 1)
            v.tensor_scalar(cs[:, 9:10], two_e, 2.0 ** -14 / H, None, ALU.mult).then_inc(s_const, 1)
            dve.wait_ge(s_chi, 2)
            dve.wait_ge(s_const, 1)
            v.tensor_copy(yv[:], q3[:]).then_inc(s_q[0], 1)

            def clip_q(step):
                v.tensor_scalar(qv[:], q3[:], 1.0 / 3.0, bounds[:, 0:1], ALU.mult, ALU.min).then_inc(s_qv, 1)
                dve.wait_ge(s_qv, step)
                v.tensor_scalar(Z[0][:, 0:CB], qv[:], bounds[:, 1:2], None, ALU.max).then_inc(s_clip, 1)

            with dve.Fori(0, T) as t:
                step = dve.snap(t + 1)
                dr = drive[:, bass.ds(t, 1), :].rearrange("p o c -> p (o c)")

                def slope_of_p(k):
                    STT(yv[:], Z[k][:, CB:2 * CB], -BETA, Z[k][:, 0:CB], ALU.mult, ALU.add).then_inc(s_y[k], 1)

                for k in range(4):
                    q, p = Z[k][:, 0:CB], Z[k][:, CB:2 * CB]
                    if k == 0:
                        dve.wait_ge(s_q[0], step)
                        clip_q(step)
                    if k in (1, 2):
                        dve.wait_ge(s_q[k], step)
                        slope_of_p(k)
                        if k == 1:
                            v.tensor_tensor(acc[:], Z[1][:], Z[0][:], ALU.subtract)
                        else:
                            STT(acc[:], Z[2][:], 2.0, acc[:], ALU.mult, ALU.add)
                    dve.wait_ge(s_tf[k], step)
                    v.tensor_tensor(tanh_hl[:, :, B:2 * B], r8(tanh_f[:]), tanh_hl[:, :, 0:B],
                                    ALU.subtract).then_inc(s_lo[k], 1)
                    if k == 0:
                        dve.wait_ge(s_clip, step)
                        dve.wait_ge(s_drv, step)
                        v.tensor_tensor(q_hd[:], dr, q, ALU.add).then_inc(s_hd[0], 1)
                        v.tensor_scalar(Z[0][:, CB:2 * CB], p3[:], bounds[:, 3:4], None, ALU.max).then_inc(s_p0, 1)
                        STT(q_hd2[:], q, 0.5, dr, ALU.mult, ALU.add)
                        dve.wait_ge(s_p0, step)
                        slope_of_p(0)
                    if k == 3:
                        dve.wait_ge(s_z4, step)
                        slope_of_p(3)
                        v.tensor_tensor(acc[:], Z[3][:], acc[:], ALU.add).then_inc(s_acc, 1)
                    dve.wait_ge(s_sq[k], step)
                    STT(cub[:], qsq[:], 3.0, q if k < 3 else q4h[:], ALU.subtract, ALU.mult)
                    if k == 3:
                        dve.wait_ge(s_acc, step)
                        v.tensor_tensor(acc_hd[:], dr, acc[:, 0:CB], ALU.add).then_inc(s_hd[3], 1)
                        STT(p3[:], yv[:], H * EPSILON, acc[:, CB:2 * CB], ALU.mult, ALU.add)
                        dve.wait_ge(s_hd[3], step)
                    STT(wv_[:], p, -H, (q_hd, q_hd, q_hd2, acc_hd)[k][:], ALU.mult, ALU.add).then_inc(s_w[k], 1)
                    if k < 3:
                        dve.wait_ge(s_y[k], step)
                        STT(Z[k + 1][:, CB:2 * CB], yv[:], (1, 1, 2)[k] * H * EPSILON, Z[0][:, CB:2 * CB],
                            ALU.mult, ALU.add).then_inc(s_p[k + 1], 1)
                    dve.wait_ge(s_w[k], step)
                    STT(psC[:, 2, 0:CB], cub[:], -(1, 1, 1, 2)[k] * H / 3, wv_[:], ALU.mult,
                        ALU.add).then_inc(s_b[k], 1)
                    if k == 2:
                        v.tensor_copy(bounds[:], cs[:, 4:8])
                    if k == 3:
                        v.tensor_scalar(p3[:], p3[:], 1.0 / 3.0, bounds[:, 2:3], ALU.mult, ALU.min)
                    dve.wait_ge(s_b[k], step)
                    dve.wait_ge(s_mm[k], step)
                    v.tensor_reduce((Z[1][:, 0:CB], Z[2][:, 0:CB], q4h[:], q3[:])[k], psS.rearrange("p s c -> p c s"),
                                    AX.X, ALU.add).then_inc(s_q[(k + 1) % 4], 1)
            dve.wait_ge(s_q[0], T + 1)
            clip_q(T + 1)
            dve.wait_ge(s_tr, 1)
            tr3 = trace[:, CB:(T + 1) * CB].rearrange("p (t c b) -> p b c t", c=C, b=B)
            dr3 = drive[:].rearrange("p t (c b) -> p b c t", b=B)
            with dve.Fori(0, B) as b:
                S["hm"].wait(dve, b, 32)
                S["hm_done"].by(v.tensor_scalar(k2t[32:33, :], k2t[32:33, :], -1.0, 1.0, ALU.mult, ALU.add))
                S["hm_done"].wait(dve, b, 1)
                S["hm_done"].by(v.tensor_scalar(k2t[32:33, :], k2t[32:33, :], -1e30, None, ALU.mult))
                S["xtr"].wait(dve, b, 0)
                for c in range(C):
                    S["x2t"].by(v.tensor_scalar(x1t[:, c], dr3[:, bass.ds(b, 1), c].rearrange("p o t -> p (o t)"),
                                                cs[:, 9:10], neg_bias[:, c:c + 1], ALU.mult, ALU.add))
                S["x2t"].wait(dve, b, 4)
                S["x2t"].by(STT(x2t, tr3[:, bass.ds(b, 1)].rearrange("p o c t -> p (o c) t"), cs[:, 0:1], x1t,
                                ALU.mult, ALU.add))
                S["xtr"].wait(dve, b, 2)
                S["x2"].by(v.tensor_copy(x2[:, 1], bank[1][:]))
                S["proj"].wait(dve, b, 1)
                S["qkv2"].wait(dve, b, 1)
                S["hm"].wait(dve, b, 32)
                S["kk"].by(v.tensor_tensor(k2t[0:DK, :], bank[2][32:32 + DK, :], hmask[:], ALU.mult))
                for qc in range(C):
                    S["sc"].wait(dve, b, qc + 1)
                    S["mx"].by(v.tensor_reduce(negmax2[:, qc:qc + 1], bank[qc % 2][:], AX.X, ALU.max, negate=True))
                S["pv"].wait(dve, b, 1)
                O = bank[3][:, 128:128 + C * 17].rearrange("p (c k) -> p c k", k=17)
                S["h2"].by(v.reciprocal(rden2[:], O[:, :, DK]))
                S["par"].wait(dve, b, 1)
                S["h2"].wait(dve, b, 1)
                S["h2"].by(v.tensor_tensor(rmask2[:], rden2[:], par[:, 0:C], ALU.mult))
                S["h2"].wait(dve, b, 2)
                S["h2"].by(v.tensor_tensor(head2[:], O[:, :, 0:DK], rmask2[:].unsqueeze(2).to_broadcast([P, C, DK]),
                                           ALU.mult))
                for tc in range(TC):
                    S["o2"].wait(dve, b, tc + 1)
                    S["x3"].by(v.tensor_tensor(x3[:, tc], bank[tc][:], x2[:, tc], ALU.add))
                S["ss"].wait(dve, b, 2)
                S["ms"].by(v.tensor_scalar(ms3[:], ss3[:], 1.0 / D, RMS_EPS, ALU.mult, ALU.add))
                S["r3"].wait(dve, b, 1)
                S["xnp"].wait(dve, b, 0)
                for tc in range(TC):
                    S["x3n"].by(v.tensor_scalar(x3n[:, tc], x3[:, tc], r3[:, tc:tc + 1], None, ALU.mult))
                for i in range(4):
                    tc, j = i // 2, i % 2
                    m = tc * 3 + j
                    S["sqr"].wait(dve, b, i + 1)
                    S["hs"].by(v.tensor_reduce(hss[:, i], sqs[i % 2][:].rearrange("p (h d) -> p h d", d=DH), AX.X, ALU.add))
                    S["hs"].wait(dve, b, i + 1)
                    S["hm3"].by(v.tensor_scalar(hms[:, i], hss[:, i], 1.0 / DH, RMS_EPS, ALU.mult, ALU.add))
                    S["hr"].wait(dve, b, i + 1)
                    if i >= 2:
                        S["qkp"].wait(dve, b, i - 1)
                    S["qkn"].by(v.tensor_tensor(qkn[i % 2][:].rearrange("p (h d) -> p h d", d=DH),
                                                bank[m][:].rearrange("p (h d) -> p h d", d=DH),
                                                hr[:, i].unsqueeze(2).to_broadcast([P, NH, DH]), ALU.mult))

                def evac(h):
                    S["et"].wait(dve, b, h + 1)
                    if h >= 2:
                        S["pv3"].wait(dve, b, h - 1)
                    S["ete"].by(v.tensor_copy(e3t[h % 2][:].rearrange("p k t -> p (k t)"), bank[2 + h % 2][:]))

                for h in range(NH):
                    S["s3"].wait(dve, b, h + 1)
                    S["m3"].by(v.tensor_reduce(negmax3[:, h % 2], bank[h % 2][:].rearrange("p (q k) -> p q k", k=T),
                                               AX.X, ALU.max, negate=True))
                    if h >= 1:
                        evac(h - 1)
                evac(NH - 1)
                S["e3"].wait(dve, b, NH)
                S["rd"].by(v.reciprocal(rden3[:], den3[:]))
                S["rd"].wait(dve, b, 1)
                S["pv3"].wait(dve, b, NH)
                for tc in range(TC):
                    S["on"].by(v.tensor_tensor(o_sb[:, tc].rearrange("p (h d) -> p h d", d=DH),
                                               bank[4 + tc][:].rearrange("p (h d) -> p h d", d=DH),
                                               rden3[:, tc].unsqueeze(2).to_broadcast([P, NH, DH]), ALU.mult))
                S["on"].wait(dve, b, 2)
                S["stored"].wait(dve, b, 0)
                for tc in range(TC):
                    S["rs"].by(v.tensor_tensor(res[:, tc], o_sb[:, tc], x3[:, tc], ALU.add))
                for tc in range(TC):
                    S["rs"].wait(dve, b, tc + 1)
                    S["op"].wait(dve, b, tc + 1)
                    S["res"].by(v.tensor_tensor(res[:, tc], bank[6 + tc][:], res[:, tc], ALU.add))

        for name, signal_ in S.items():
            assert name in ("hm", "stored") or signal_.n == signal_.per, name


_INS = ["x", "cond_2048", "L0_cond_b", "L1_cond_coupling", "L1_cond_bias", "L2_cond_Wq", "L2_cond_Wk", "L2_cond_Wv",
        "L2_cond_Wo", "L3_cond_W_emb", "L3_cond_b_emb", "L3_cond_g_norm", "L3_cond_W_qkv", "L3_cond_g_q",
        "L3_cond_g_k", "L3_cond_W_out"]


def kernel(**inputs):
    import numpy as np
    import concourse.bacc as bacc
    from concourse import mybir
    from concourse.bass_utils import run_bass_kernel_spmd

    nc = bacc.Bacc("TRN2", target_bir_lowering=False, num_devices=1)
    arrays, args = {}, []
    for name in _INS:
        a = np.ascontiguousarray(inputs[name])
        arrays[f"in_{name}"] = a
        args.append(nc.dram_tensor(f"in_{name}", a.shape, mybir.dt.from_np(a.dtype), kind="ExternalInput").ap())
    args.append(nc.dram_tensor("out", inputs["x"].shape, mybir.dt.float32, kind="ExternalOutput").ap())
    build(nc, *args)
    r = run_bass_kernel_spmd(nc, [arrays], core_ids=[0])
    return r.results[0]["out"]
```

```python
from contextlib import ExitStack

import concourse.bass as bass
from concourse import mybir

F32 = mybir.dt.float32
F16 = mybir.dt.float16
I32 = mybir.dt.int32
ALU = mybir.AluOpType
ACT = mybir.ActivationFunctionType
AX = mybir.AxisListType
RMAX = bass.bass_isa.ReduceOp.max

P = 128
DT = 0.01
H = DT / 2
EPSILON, ALPHA, BETA, CLAMP = 0.08, 0.7, 0.8, 20.0
SHIFT = ALPHA / BETA
RMS_EPS = 1e-6
BIG = 3.0e38


class Signal:

    def __init__(self, sem, per, base=0):
        self.sem, self.per, self.base, self.n = sem, per, base, 0

    def by(self, ins):
        self.n += 1
        ins.then_inc(self.sem, 1)
        return self.n

    def wait(self, eng, turn, n):
        eng.wait_ge(self.sem, turn * self.per + (self.base + n))

    def closed(self):
        assert self.n == self.per, (self.n, self.per)


def build(nc, x, cond, L0_b, coupling, L1_bias, Wq, Wk, Wv, Wo, W_emb, b_emb, g_norm, W_qkv, g_q, g_k,
          W_out, out):
    B, T, D = x.shape
    TAPS = cond.shape[0]
    C = D // P
    TC = T // P
    CB = C * B
    HEADS, DK = Wq.shape[0], Wq.shape[2]
    DH = g_q.shape[0]
    NH = D // DH
    HPC = P // DH
    SCALE2 = float(DK) ** -0.5
    SCALE3 = float(DH) ** -0.5
    assert (B, C, TC, TAPS, DK, DH) == (8, 4, 2, 8, 16, 32)

    with ExitStack() as ctx:
        def sb(name, shape, dt=F32):
            return ctx.enter_context(nc.sbuf_tensor(name, shape, dt))

        def sem(name):
            return ctx.enter_context(nc.semaphore(name))

        padded = sb("padded_x", [P, (T + TAPS - 1) * CB])
        drive = sb("drive", [P, T, CB])
        trace = sb("trace", [P, (T + 1) * CB])
        c_hi = sb("c_hi", [P, C, D], F16)
        c_lo = sb("c_lo", [P, C, D], F16)
        wqkv = sb("wqkv", [P, C, 3 * D])
        wout = sb("wout", [P, C, D])
        ident = sb("ident", [P, P])
        coup = trace[:, 0:C * D].rearrange("p (c m) -> p c m", c=C)
        coup_t = trace[:, C * D:2 * C * D].rearrange("p (c n) -> p c n", c=C)
        wemb = trace[:, 2 * C * D:4 * C * D].rearrange("p (c n) -> p c n", c=C)
        tiles = padded[:, 0:8 * TC * D].rearrange("p (i t d) -> p i t d", i=8, t=TC)
        x2t = tiles[:, 0].rearrange("p t d -> p (t d)").rearrange("p (c t) -> p c t", c=C)
        x2, x3, x3n, o_sb, res, x1t = (tiles[:, i] for i in range(1, 7))
        x1t = x1t.rearrange("p t d -> p (t d)").rearrange("p (c t) -> p c t", c=C)
        o_t = tiles[:, 7].rearrange("p t d -> p (t d)").rearrange("p (c t) -> p c t", c=C)

        rows = sb("rows", [16, D])
        cols = sb("cols", [P, C, 16])
        taps = sb("taps", [P, TAPS, CB])
        conv_bias = sb("conv_bias", [P, CB])
        h_sigma = sb("h_sigma", [P, CB])
        neg_bias = sb("neg_bias", [P, C])
        cmax = sb("cmax", [P, 2])
        cmaxb = sb("bias_sum", [P, C])
        ebits = sb("ebits", [P, 2], I32)
        pow2 = sb("pow2", [P, 2])
        cs = sb("consts", [P, 10])
        bounds = sb("bounds", [P, 4])
        gains = sb("gains", [P, HPC + 1])
        of_head = sb("of_head", [P, HPC])
        Z = [sb(f"stage{k}_qp", [P, 2 * CB]) for k in range(4)]
        tanh_hl = sb("tanh_hl", [P, C, 2 * B], F16)
        tanh_f = sb("tanh_f", [P, CB])
        qsq = sb("qsq", [P, CB])
        yv = sb("q_minus_beta_p", [P, CB])
        wv_ = sb("linear_part", [P, CB])
        cub = sb("cubic_part", [P, CB])
        q_hd = sb("q_plus_drive", [P, CB])
        q_hd2 = sb("half_q_plus_drive", [P, CB])
        acc_hd = sb("acc_q_drive", [P, CB])
        acc = sb("acc_qp", [P, 2 * CB])
        acc_d = sb("acc_plus_drive", [P, CB])
        beta_p = sb("minus_beta_p", [P, CB])
        q3 = sb("q3_sum", [P, CB])
        qv = sb("q_unclipped", [P, CB])
        p3 = sb("p3_sum", [P, CB])
        q4h = sb("stage3_half_q", [P, CB])
        prod = sb("prod", [P, TAPS * CB])
        half = sb("half_sum", [P, 4 * CB])
        quart = sb("quarter_sum", [P, 2 * CB])
        conv = sb("conv", [P, CB])
        xb = sb("x_plus_bias", [P, CB])
        dsum = sb("dsum", [P, CB])
        wqk2 = sb("wqk2", [P, TC, P])
        wv2 = sb("wv2", [P, TC, DK])
        wo2 = sb("wo2", [P, 2, T])
        fold = sb("fold", [P, DK])
        wo_sum = sb("wo_sum", [DK, T])
        params = sb("params", [P, B, 12])
        par = sb("par", [P, 12])
        hmask = sb("hmask", [DK, D])
        q2t = sb("q2t", [P, D])
        k2t = sb("k2t", [P, D])
        v2 = sb("v2", [P, C, DK + 1])
        negmax2 = sb("negmax2", [P, C])
        e2 = sb("e2", [P, C, D])
        rden2 = sb("rden2", [P, C])
        rmask2 = sb("rmask2", [P, C])
        head2 = sb("head2", [P, C, DK])
        head2t = sb("head2t", [DK, D])
        ss3 = sb("ss3", [P, TC])
        ms3 = sb("ms3", [P, TC])
        r3 = sb("r3", [P, TC])
        xnt = sb("xnt", [P, C, T])
        sqs = [sb(f"sq_{i}", [P, D]) for i in range(2)]
        hss = sb("head_ss", [P, 4, NH])
        hms = sb("head_ms", [P, 4, NH])
        hr = sb("head_r", [P, 4, NH])
        halves = sb("minus_half", [P, NH])
        qkn = [sb(f"qkn_{i}", [P, D]) for i in range(2)]
        qth = [c_.rearrange("p c m -> p (c m)").bitcast(F32).rearrange("p (c t) -> p c t", c=C)
               for c_ in (c_hi[:], c_lo[:])] + [sb(f"qt_{i}", [P, C, T]) for i in (2, 3)]
        kt = sb("kt", [P, C, T])
        v3h = sb("v3_hi", [P, TC, D], F16)
        v3l = sb("v3_lo", [P, TC, D], F16)
        vmax = sb("v_bound_parts", [P, 4])
        wvmax = sb("wv_max", [P, C])
        vbits = sb("v_exponent", [P, 2], I32)
        vscale = sb("v_scale", [P, 2])
        negmax3 = sb("negmax3", [P, 2, TC])
        e3 = [sb(f"e3_{i}", [P, TC, T]) for i in range(2)]
        e3t_hi = [sb(f"e3t_hi_{i}", [P, TC, T], F16) for i in range(2)]
        e3t_lo = [sb(f"e3t_lo_{i}", [P, TC, T], F16) for i in range(2)]
        den3 = sb("den3", [P, TC, NH])
        rden3 = sb("rden3", [P, TC, NH])
        xl = [e2[:, j] for j in range(4)]

        bank = [ctx.enter_context(nc.psum_tensor(f"bank{i}", [P, 512], F32)) for i in range(5)]
        psC = ctx.enter_context(nc.psum_tensor("psC", [P, 4, 256], F32))
        bank += [psC[:, 0:2, :].rearrange("p a b -> p (a b)"), psC[:, 2:4, :].rearrange("p a b -> p (a b)")]
        bank.append(ctx.enter_context(nc.psum_tensor("bank7", [P, 512], F32)))
        psS = psC[:, 0:3, 0:CB]

        s_ld = sem("weights_loaded")
        s_lc = sem("coupling_loaded")
        s_lr = sem("rows_loaded")
        s_rowz = sem("rows_cleared")
        s_id = sem("identity_ready")
        s_pool = sem("pool_chain")
        s_colp = sem("cols_transposed")
        s_cols = sem("cols_ready")
        s_cm = sem("coupling_max")
        s_cma = sem("coupling_max_all")
        s_ct = sem("coupling_transposed")
        s_cte = sem("coupling_evacuated")
        s_vec0 = sem("vector_chain_prep")
        s_par = sem("conv_params_ready")
        s_const = sem("consts_ready")
        s_chi = sem("c_hi_ready")
        s_emb = sem("emb_products")
        s_prm = sem("params_ready")
        s_fold = sem("fold_ready")
        s_wos = sem("wo_products")
        s_xl = [sem(f"x_loaded{j}") for j in range(4)]
        s_xt = sem("x_transposed")
        s_xe = [sem(f"x_evacuated{j}") for j in range(2)]
        s_pad = sem("pad_cleared")
        s_drv = sem("drive_ready")
        s_q = [sem(f"stage{k}_q_ready") for k in range(4)]
        s_hi = [sem(f"stage{k}_tanh_hi") for k in range(4)]
        s_tf = [sem(f"stage{k}_tanh_f") for k in range(4)]
        s_sq = [sem(f"stage{k}_q_squared") for k in range(4)]
        s_lo = [sem(f"stage{k}_tanh_lo") for k in range(4)]
        s_mm = [sem(f"stage{k}_coupling") for k in range(4)]
        s_pv = sem("p_bounded_above")
        s_qv = sem("q_bounded_above")
        s_clip = sem("q_clipped")
        s_p0 = sem("stage0_p")
        s_p = [None] + [sem(f"stage{k}_p") for k in range(1, 4)]
        s_y = [sem(f"stage{k}_y") for k in range(4)]
        s_acc = sem("stage2_acc")
        s_accd = sem("acc_for_stage3")
        s_hd = [sem("stage0_q_plus_drive"), None, None, sem("stage3_acc_plus_drive")]
        s_w = [sem(f"stage{k}_linear") for k in range(4)]
        s_b = [sem(f"stage{k}_addend") for k in range(4)]
        s_tr = sem("trace_done")
        s_vm = sem("v_bound_parts_ready")
        s_vs = sem("v_scale_ready")
        s_vma = sem("v_bound_parts_all")

        block = ctx.enter_context(nc.Block())

        def r8(a):
            return a.rearrange("p (c b) -> p c b", b=B)

        def signal(name, per):
            return Signal(sem(name), per, 1)

        def tail_signals():
            return dict(
                hm=signal("hmask_loaded", 32), hm_done=signal("mask_row_ready", 2),
                par=signal("batch_params", 1),
                x2t=signal("x2t_ready", 5), xtr=signal("x2_transposed", 2), x2=signal("x2_ready", 2),
                proj=signal("l2_proj", 2), qkv2=signal("l2_qkv_ready", 2),
                kk=signal("l2_keys_ready", 1), sc=signal("l2_scores", 4), mx=signal("l2_max", 4), mt=signal("l2_max_row", 1),
                mrow=signal("l2_max_ready", 1), st=signal("l2_scores_t", 4), e2=signal("l2_exp", 4),
                pv=signal("l2_pv", 1), h2=signal("l2_head", 3), h2t=signal("l2_head_t", 1),
                h2e=signal("l2_head_t_ready", 1), o2=signal("l2_out", 2), x3=signal("x3_ready", 2),
                ss=signal("x3_squares", 2), ms=signal("x3_mean", 1), r3=signal("x3_rms", 1),
                x3n=signal("x3_normed", 2), xnp=signal("xn_transposed", 2), xnt=signal("xnt_ready", 4),
                qkv=signal("l3_qkv", 6), sqr=signal("qk_squares", 4), hs=signal("qk_sums", 4),
                hm3=signal("qk_means", 4), hr=signal("qk_rms", 4), qkn=signal("qk_normed", 4),
                v3=signal("v3_hi_ready", 2), v3l=signal("v3_lo_ready", 2), qkp=signal("qk_transposed", 4), qkt=signal("qkt_ready", 6), qkt2=signal("qkt_ready_too", 4),
                s3=signal("l3_scores", NH), m3=signal("l3_max", NH), e3=signal("l3_exp", NH),
                et=signal("l3_probs_t", NH), eth=signal("l3_probs_t_hi", NH), etl=signal("l3_probs_t_lo", NH), pv3=signal("l3_pv", NH),
                rd=signal("l3_rden", 2), on=signal("l3_o_ready", 2), ot=signal("l3_o_t", 2),
                ote=signal("l3_o_t_ready", 2), op=signal("l3_out", 2), rs=signal("res_part", 2),
                res=signal("res_ready", 2), stored=signal("stored", 32))

        S = tail_signals()

        @block.sync
        def _(sp):
            for signal_ in (s_xt, *s_xe, *(one_.sem for one_ in S.values())):
                sp.sem_inc(signal_, 1)
            sp.dma_start(coup, coupling.rearrange("(c p) m -> p c m", p=P)).then_inc(s_lc, 16)
            one = lambda a: a.rearrange("(o d) -> o d", o=1)
            sp.dma_start(rows[0:B, :], cond).then_inc(s_lr, 16)
            for r, v in ((8, one(L0_b)), (9, one(L1_bias)), (10, one(g_norm)), (11, one(b_emb[0:D])),
                         (12, one(b_emb[D:2 * D])), (15, one(L0_b))):
                sp.dma_start(rows[r:r + 1, :], v).then_inc(s_lr, 16)
            for r, v in ((13, g_q), (14, g_k)):
                sp.dma_start(rows[r:r + 1, :].rearrange("o (h d) -> o h d", d=DH),
                             one(v).unsqueeze(1).to_broadcast([1, NH, DH])).then_inc(s_lr, 16)
            with sp.Fori(0, B // 2) as i:
                for j in range(4):
                    sp.wait_ge(s_xt, i * 4 + 1)
                    sp.dma_start(xl[j], x[bass.ds(i * 2 + j // 2, 1), (j % 2) * P:(j % 2 + 1) * P, :]
                                 .rearrange("o t d -> (o t) d")).then_inc(s_xl[j], 16)
            sp.dma_start(wemb, W_emb.rearrange("(c p) n -> p c n", p=P)).then_inc(s_ld, 16)
            sp.wait_ge(s_rowz, 1)
            sp.dma_start(wqk2[:, :, 0:DK], Wq[1].rearrange("(c p) k -> p c k", p=P)).then_inc(s_ld, 16)
            sp.dma_start(wqk2[:, :, 32:32 + DK], Wk[1].rearrange("(c p) k -> p c k", p=P)).then_inc(s_ld, 16)
            sp.dma_start(wv2[:], Wv[1].rearrange("(c p) k -> p c k", p=P)).then_inc(s_ld, 16)
            sp.dma_start(wo2[:], Wo.rearrange("(c p) t -> p c t", p=P)).then_inc(s_ld, 16)
            sp.dma_start(wqkv[:], W_qkv.rearrange("(c p) n -> p c n", p=P)).then_inc(s_ld, 16)
            sp.dma_start(wout[:], W_out.rearrange("(c p) n -> p c n", p=P)).then_inc(s_ld, 16)
            with sp.Fori(0, B) as b:
                S["st"].wait(sp, b, 0)
                row = cond[bass.ds(b, 1), :]
                sp.dma_start(hmask[:], row.to_broadcast([DK, D])).then_inc(S["hm"].sem, 16)
                sp.dma_start(k2t[32:33, :], row).then_inc(S["hm"].sem, 16)
                for tc in range(TC):
                    S["res"].wait(sp, b, tc + 1)
                    sp.dma_start(out[bass.ds(b, 1), tc * P:(tc + 1) * P, :].rearrange("o t d -> (o t) d"),
                                 res[:, tc]).then_inc(S["stored"].sem, 16)
            sp.wait_ge(S["stored"].sem, 32 * B + 1)

        @block.gpsimd
        def _(pool):
            g = nc.gpsimd
            g.memset(ident[:], 0.0).then_inc(s_pool, 1)
            pool.wait_ge(s_pool, 1)
            g.affine_select(out=ident[:], in_=ident[:], compare_op=ALU.not_equal, fill=1.0, base=0,
                            pattern=[[-1, P]], channel_multiplier=1).then_inc(s_id, 1)
            g.memset(wqk2[:], 0.0).then_inc(s_rowz, 1)
            g.memset(padded[:, 0:(TAPS - 1) * CB], 0.0).then_inc(s_pad, 1)
            g.memset(halves[:], -0.5)
            g.memset(q2t[:], 0.0)
            g.memset(k2t[:], 0.0)
            g.memset(v2[:], 1.0).then_inc(s_pool, 1)
            pool.wait_ge(s_pool, 2)
            g.memset(q2t[32:33, :], 1.0)
            g.memset(k2t[64:65, :], 1.0).then_inc(s_pool, 1)
            pool.wait_ge(s_pool, 3)
            pool.wait_ge(s_cm, 1)
            g.partition_all_reduce(cmax[:, 1:2], cmax[:, 0:1], P, RMAX).then_inc(s_cma, 1)
            pool.wait_ge(s_par, 1)
            pool.wait_ge(s_pool, 3)
            pool.wait_ge(s_pad, 1)
            for e in s_xe:
                pool.wait_ge(e, B + 1)
            ch = Signal(s_pool, 6, 3)
            with pool.Fori(0, T) as t:
                ch.wait(pool, t, 0)
                win = padded[:, bass.ds(t * CB, TAPS * CB)]
                g.tensor_tensor(prod[:], win, taps[:].rearrange("p k c -> p (k c)"), ALU.mult).then_inc(s_pool, 1)
                g.tensor_tensor(xb[:], padded[:, bass.ds(t * CB + (TAPS - 1) * CB, CB)], conv_bias[:],
                                ALU.add).then_inc(s_pool, 1)
                ch.wait(pool, t, 2)
                g.tensor_tensor(half[:], prod[:, 0:4 * CB], prod[:, 4 * CB:8 * CB], ALU.add).then_inc(s_pool, 1)
                ch.wait(pool, t, 3)
                g.tensor_tensor(quart[:], half[:, 0:2 * CB], half[:, 2 * CB:4 * CB], ALU.add).then_inc(s_pool, 1)
                ch.wait(pool, t, 4)
                g.tensor_tensor(conv[:], quart[:, 0:CB], quart[:, CB:2 * CB], ALU.add).then_inc(s_pool, 1)
                ch.wait(pool, t, 5)
                g.tensor_tensor(dsum[:], conv[:], xb[:], ALU.add).then_inc(s_pool, 1)
                ch.wait(pool, t, 6)
                g.tensor_tensor(drive[:, bass.ds(t, 1), :].rearrange("p o c -> p (o c)"), dsum[:], h_sigma[:],
                                ALU.mult).then_inc(s_drv, 1)
            pool.wait_ge(s_prm, 1)
            pool.wait_ge(s_vm, 1)
            for i in range(2):
                g.partition_all_reduce(vmax[:, 2 + i:3 + i], vmax[:, i:i + 1], P, RMAX).then_inc(s_vma, 1)
            with pool.Fori(0, B) as b:
                S["xnt"].wait(pool, b, 0)
                S["h2"].wait(pool, b, 0)
                S["par"].by(g.tensor_copy(par[:], params[:, bass.ds(b, 1), :].rearrange("p o c -> p (o c)")))
                S["ms"].wait(pool, b, 1)
                S["r3"].by(g.tensor_tensor(r3[:], ms3[:], halves[:, 0:TC], ALU.pow))
                for i in range(4):
                    S["hm3"].wait(pool, b, i + 1)
                    S["hr"].by(g.tensor_tensor(hr[:, i], hms[:, i], halves[:], ALU.pow))

        @block.scalar
        def _(act):
            a = nc.scalar
            with act.Fori(0, B // 2) as i:
                for j in (1, 3):
                    act.wait_ge(s_xt, i * 4 + (j + 2))
                    bb, tc = i * 2 + j // 2, j % 2
                    dst = padded[:, (TAPS - 1 + tc * P) * CB:(TAPS - 1 + (tc + 1) * P) * CB] \
                        .rearrange("p (t c b) -> p b c t", c=C, b=B)
                    a.copy(dst[:, bass.ds(bb, 1)].rearrange("p o c t -> p (o c) t"),
                           bank[j][:].rearrange("p (c t) -> p c t", c=C)).then_inc(s_xe[1], 1)
            a.preload_act_table(ACT.Tanh)
            act.wait_ge(s_const, 1)
            scale = []
            for j in range(3):
                reg = act.alloc_register(f"tanh_scale{j}")
                act.reg_load(reg, cs[0:1, j:j + 1].bitcast(I32))
                scale.append(reg)
            with act.Fori(0, T) as t:
                step = act.snap(t + 1)
                for k in range(4):
                    src, s = ((q3[:], scale[2]), (Z[1][:, 0:CB], scale[0]), (Z[2][:, 0:CB], scale[0]),
                              (q4h[:], scale[1]))[k]
                    act.wait_ge(s_q[k], step)
                    a.activation(tanh_hl[:, :, 0:B], r8(src), ACT.Tanh, scale=s).then_inc(s_hi[k], 1)
                    a.activation(tanh_f[:], src, ACT.Tanh, scale=s).then_inc(s_tf[k], 1)
                    if k == 0:
                        act.wait_ge(s_clip, step)
                        a.activation(qsq[:], Z[0][:, 0:CB], ACT.Square, scale=scale[0]).then_inc(s_sq[0], 1)
                        a.activation(trace[:, bass.ds(t * CB, CB)], Z[0][:, 0:CB], ACT.Copy)
                    else:
                        a.activation(qsq[:], src, ACT.Square, scale=s).then_inc(s_sq[k], 1)
            act.wait_ge(s_clip, T + 1)
            a.activation(trace[:, T * CB:(T + 1) * CB], Z[0][:, 0:CB], ACT.Copy).then_inc(s_tr, 1)
            a.preload_act_table(ACT.Exp)
            act.wait_ge(s_vs, 1)
            with act.Fori(0, B) as b:
                S["xtr"].wait(act, b, 1)
                S["o2"].wait(act, b, 0)
                S["x3"].wait(act, b, 0)
                S["x2"].by(a.copy(x2[:, 0], bank[0][:]))
                S["proj"].wait(act, b, 1)
                S["st"].wait(act, b, 0)
                S["qkv2"].by(a.activation(q2t[0:DK, :], bank[2][0:DK, :], ACT.Copy, scale=SCALE2))
                S["proj"].wait(act, b, 2)
                S["pv"].wait(act, b, 0)
                S["qkv2"].by(a.copy(v2[:, :, 0:DK], bank[3][:, 0:C * DK].rearrange("p (c k) -> p c k", c=C)))
                S["mt"].wait(act, b, 1)
                S["mrow"].by(a.copy(q2t[64:65, :], bank[2][0:1, :]))
                for kc in range(C):
                    S["st"].wait(act, b, kc + 1)
                    S["e2"].by(a.activation(e2[:, kc], bank[kc % 2][:], ACT.Exp))
                S["h2t"].wait(act, b, 1)
                S["h2e"].by(a.copy(head2t[:], bank[2][0:DK, :]))
                for tc in range(TC):
                    S["x3"].wait(act, b, tc + 1)
                    S["ss"].by(a.activation(sqs[tc][:], x3[:, tc], ACT.Square, accum_out=ss3[:, tc:tc + 1]))
                S["par"].wait(act, b, 1)
                for dc in range(C):
                    if dc % 2 == 0:
                        S["xnp"].wait(act, b, dc // 2 + 1)
                    S["xnt"].by(a.activation(xnt[:, dc], bank[2 + dc // 2][:, (dc % 2) * T:(dc % 2 + 1) * T],
                                             ACT.Identity, bias=par[:, 8 + dc:9 + dc], scale=par[:, 4 + dc:5 + dc]))
                for tc in range(TC):
                    for j in range(3):
                        m = tc * 3 + j
                        S["qkv"].wait(act, b, m + 1)
                        if j < 2:
                            i = tc * 2 + j
                            if i >= 2:
                                S["hs"].wait(act, b, i - 1)
                            S["sqr"].by(a.activation(sqs[i % 2][:], bank[m][:], ACT.Square))
                        else:
                            S["pv3"].wait(act, b, 0)
                            S["v3"].by(a.activation(v3h[:, tc], bank[m][:], ACT.Copy, scale=vscale[:, 0:1]))
                for i in range(4):
                    tc, j = i // 2, i % 2
                    S["qkp"].wait(act, b, i + 1)
                    for r in ((0, 1), (HPC,))[j]:
                        S["qkt"].by(a.activation((*qth, kt)[r][:, :, tc * P:(tc + 1) * P],
                                                 bank[6 + i % 2][:].rearrange("p (c t) -> p c t", c=C), ACT.Copy,
                                                 scale=gains[:, r:r + 1]))

                def exps(h):
                    S["m3"].wait(act, b, h + 1)
                    if h >= 2:
                        S["et"].wait(act, b, h - 1)
                    for tc in range(TC):
                        e = a.activation(e3[h % 2][:, tc], bank[h % 2][:, tc * T:(tc + 1) * T], ACT.Exp,
                                         bias=negmax3[:, h % 2, tc:tc + 1],
                                         accum_out=den3[:, tc, h:h + 1])
                    S["e3"].by(e)

                exps(0)
                exps(1)
                for h in range(NH):
                    S["et"].wait(act, b, h + 1)
                    if h >= 2:
                        S["pv3"].wait(act, b, h - 1)
                        S["etl"].wait(act, b, h - 1)
                    S["eth"].by(a.copy(e3t_hi[h % 2][:].rearrange("p k t -> p (k t)"), bank[2 + h % 2][:]))
                    if h + 2 < NH:
                        exps(h + 2)
                for tc in range(TC):
                    S["ot"].wait(act, b, tc + 1)
                    S["ote"].by(a.copy(o_t[:, 2 * tc:2 * tc + 2], bank[tc][:].rearrange("p (c t) -> p c t", c=2)))

        @block.tensor
        def _(pe):
            mm = nc.tensor.matmul
            tr = nc.tensor.transpose
            pe.wait_ge(s_id, 1)
            pe.wait_ge(s_lr, 16 * 9)
            for c in range(C):
                ins = tr(bank[4][:, c * 16:(c + 1) * 16], rows[:, c * P:(c + 1) * P], ident[0:16, 0:16])
            ins.then_inc(s_colp, 1)
            with pe.Fori(0, B // 2) as i:
                for j in range(4):
                    pe.wait_ge(s_xl[j], i * 16 + 16)
                    pe.wait_ge(s_xe[j % 2], i * 2 + (j // 2 + 1))
                    for c in range(C):
                        ins = tr(bank[j][:, c * P:(c + 1) * P], xl[j][:, c * P:(c + 1) * P], ident[:])
                    ins.then_inc(s_xt, 1)
            pe.wait_ge(s_lc, 16)
            for mc in range(C):
                pe.wait_ge(s_xe[mc % 2], B + 1)
                for n in range(C):
                    ins = tr(bank[mc][:, n * P:(n + 1) * P], coup[:, n, mc * P:(mc + 1) * P], ident[:])
                ins.then_inc(s_ct, 1)
            pe.wait_ge(s_ld, 16 * 7)
            pe.wait_ge(s_cols, 1)
            for n in range(2 * C):
                for c in range(C):
                    ins = mm(bank[4][:, 64 + n * B:64 + (n + 1) * B], wemb[:, c, n * P:(n + 1) * P], cols[:, c, 0:B],
                             start=(c == 0), stop=(c == C - 1))
            ins.then_inc(s_emb, 1)
            pe.wait_ge(s_fold, 1)
            for c in range(2):
                ins = mm(bank[7][0:DK, 0:T], fold[:], wo2[:, c], start=(c == 0), stop=(c == 1))
            ins.then_inc(s_wos, 1)

            pe.wait_ge(s_chi, 2)
            with pe.Fori(0, T) as t:
                step = pe.snap(t + 1)
                for k in range(4):
                    pe.wait_ge(s_hi[k], step)
                    for kc in range(C):
                        for m in range(C):
                            mm(psC[:, 0, m * B:(m + 1) * B], c_lo[:, kc, m * P:(m + 1) * P], tanh_hl[:, kc, 0:B],
                               start=(kc == 0 and m == 0), stop=False, skip_group_check=True)
                    pe.wait_ge(s_lo[k], step)
                    for m in range(C):
                        for kc in range(C):
                            ins = mm(psC[:, 0:2, m * B:(m + 1) * B], c_hi[:, kc, m * P:(m + 1) * P],
                                     tanh_hl[:, kc, :].rearrange("p (s b) -> p s b", s=2),
                                     start=False, stop=(kc == C - 1 and m == C - 1), skip_group_check=True)
                    ins.then_inc(s_mm[k], 1)
            pe.wait_ge(s_q[0], T + 1)
            with pe.Fori(0, B) as b:
                for tc in range(TC):
                    S["x2t"].wait(pe, b, 5)
                    if tc == 0:
                        S["ote"].wait(pe, b, 0)
                        S["res"].wait(pe, b, 0)
                    for c in range(C):
                        ins = tr(bank[tc][:, c * P:(c + 1) * P], x2t[:, c, tc * P:(tc + 1) * P], ident[:])
                    S["xtr"].by(ins)
                S["x2"].wait(pe, b, 2)
                for tc in range(TC):
                    ins = mm(bank[2][:], wqk2[:, tc], x2[:, tc], start=(tc == 0), stop=(tc == TC - 1))
                S["proj"].by(ins)
                for c in range(C):
                    for tc in range(TC):
                        ins = mm(bank[3][:, c * DK:(c + 1) * DK], x2[:, tc, c * P:(c + 1) * P], wv2[:, tc],
                                 start=(tc == 0), stop=(tc == TC - 1))
                S["proj"].by(ins)
                S["qkv2"].wait(pe, b, 2)
                S["kk"].wait(pe, b, 1)
                S["hm_done"].wait(pe, b, 2)
                for qc in range(C):
                    if qc >= 2:
                        S["mx"].wait(pe, b, qc - 1)
                    S["sc"].by(mm(bank[qc % 2][:], q2t[0:64, qc * P:(qc + 1) * P], k2t[0:64, :], start=True, stop=True))
                S["mx"].wait(pe, b, 4)
                for qc in range(C):
                    ins = tr(bank[2][0:1, qc * P:(qc + 1) * P], negmax2[:, qc:qc + 1], ident[:])
                S["mt"].by(ins)
                S["mrow"].wait(pe, b, 1)
                for kc in range(C):
                    if kc >= 2:
                        S["e2"].wait(pe, b, kc - 1)
                    S["st"].by(mm(bank[kc % 2][:], k2t[0:65, kc * P:(kc + 1) * P], q2t[0:65, :], start=True, stop=True))
                S["e2"].wait(pe, b, 4)
                for qc in range(C):
                    for kc in range(C):
                        ins = mm(bank[3][:, 128 + qc * 17:128 + (qc + 1) * 17], e2[:, kc, qc * P:(qc + 1) * P], v2[:, kc],
                                 start=(kc == 0), stop=(kc == C - 1))
                S["pv"].by(ins)
                S["h2"].wait(pe, b, 3)
                for qc in range(C):
                    ins = tr(bank[2][0:DK, qc * P:(qc + 1) * P], head2[:, qc], ident[:])
                S["h2t"].by(ins)
                S["h2e"].wait(pe, b, 1)
                for tc in range(TC):
                    S["o2"].by(mm(bank[tc][:], wo_sum[:, tc * P:(tc + 1) * P], head2t[:], start=True, stop=True))
                for dc in range(C):
                    for tc in range(TC):
                        S["x3n"].wait(pe, b, tc + 1)
                        ins = tr(bank[2 + dc // 2][:, (dc % 2) * T + tc * P:(dc % 2) * T + (tc + 1) * P],
                                 x3n[:, tc, dc * P:(dc + 1) * P], ident[:])
                    if dc % 2:
                        S["xnp"].by(ins)
                S["xnt"].wait(pe, b, 4)
                for tc in range(TC):
                    for j in range(3):
                        m = tc * 3 + j
                        for dc in range(C):
                            ins = mm(bank[m][:], xnt[:, dc, tc * P:(tc + 1) * P], wqkv[:, dc, j * D:(j + 1) * D],
                                     start=(dc == 0), stop=(dc == C - 1))
                        S["qkv"].by(ins)
                for i in range(4):
                    S["qkn"].wait(pe, b, i + 1)
                    if i >= 2:
                        S["qkt"].wait(pe, b, i)
                        S["qkt2"].wait(pe, b, 2)
                    for c in range(C):
                        ins = tr(bank[6 + i % 2][:, c * P:(c + 1) * P], qkn[i % 2][:, c * P:(c + 1) * P], ident[:])
                    S["qkp"].by(ins)
                S["qkt"].wait(pe, b, 6)
                S["qkt2"].wait(pe, b, 4)

                def scores(h):
                    c = h // HPC
                    if h >= 2:
                        S["e3"].wait(pe, b, h - 1)
                    for tc in range(TC):
                        ins = mm(bank[h % 2][:, tc * T:(tc + 1) * T], qth[h % HPC][:, c, tc * P:(tc + 1) * P],
                                 kt[:, c, :], start=True, stop=True)
                    S["s3"].by(ins)

                def turn(h):
                    S["e3"].wait(pe, b, h + 1)
                    if h >= 2:
                        S["etl"].wait(pe, b, h - 1)
                        S["eth"].wait(pe, b, h - 1)
                    for kc in range(TC):
                        for tc in range(TC):
                            ins = tr(bank[2 + h % 2][:, kc * T + tc * P:kc * T + (tc + 1) * P],
                                     e3[h % 2][:, tc, kc * P:(kc + 1) * P], ident[:])
                    S["et"].by(ins)

                def pv(h):
                    S["etl"].wait(pe, b, h + 1)
                    for tc in range(TC):
                        for n, (kc, e, vv) in enumerate((kc, e, vv) for e, vv in
                                                        ((e3t_lo, v3h), (e3t_hi, v3l), (e3t_hi, v3h))
                                                        for kc in range(TC)):
                            ins = mm(bank[4 + tc][:, h * DH:(h + 1) * DH], e[h % 2][:, kc, tc * P:(tc + 1) * P],
                                     vv[:, kc, h * DH:(h + 1) * DH], start=(n == 0), stop=(n == 3 * TC - 1))
                    S["pv3"].by(ins)

                S["v3l"].wait(pe, b, 2)
                scores(0)
                scores(1)
                for h in range(NH):
                    if h + 2 < NH:
                        scores(h + 2)
                    if h >= 2:
                        pv(h - 2)
                    turn(h)
                pv(NH - 2)
                pv(NH - 1)
                for dc in range(C):
                    for tc in range(TC):
                        S["on"].wait(pe, b, tc + 1)
                        ins = tr(bank[dc // 2][:, (dc % 2) * T + tc * P:(dc % 2) * T + (tc + 1) * P],
                                 o_sb[:, tc, dc * P:(dc + 1) * P], ident[:])
                    if dc % 2:
                        S["ot"].by(ins)
                S["ote"].wait(pe, b, 2)
                for tc in range(TC):
                    for dc in range(C):
                        ins = mm(bank[6 + tc][:], o_t[:, dc, tc * P:(tc + 1) * P], wout[:, dc], start=(dc == 0),
                                 stop=(dc == C - 1))
                    S["op"].by(ins)

        @block.vector
        def _(dve):
            v = nc.vector
            STT = v.scalar_tensor_tensor
            chain = [0]

            def link(ins):
                chain[0] += 1
                ins.then_inc(s_vec0, 1)
                dve.wait_ge(s_vec0, chain[0])

            dve.wait_ge(s_lc, 16)
            v.tensor_reduce(cmax[:, 0:1], coup.rearrange("p c m -> p (c m)"), AX.X, ALU.max,
                            apply_absolute_value=True).then_inc(s_cm, 1)
            dve.wait_ge(s_colp, 1)
            v.tensor_copy(cols[:].rearrange("p c r -> p (c r)"), bank[4][:, 0:64]).then_inc(s_cols, 1)
            dve.wait_ge(s_cols, 1)
            dve.wait_ge(s_cma, 1)
            link(v.tensor_scalar(pow2[:, 0:1], cmax[:, 1:2], H, 2.0 ** -40, ALU.mult, ALU.max))
            link(v.tensor_scalar(pow2[:, 0:1], pow2[:, 0:1], 2.0 ** 60, None, ALU.min))
            link(v.tensor_scalar(ebits[:, 0:1], pow2[:, 0:1].bitcast(I32), 0x7F800000, None, ALU.bitwise_and))
            link(v.tensor_scalar(ebits[:, 1:2], ebits[:, 0:1], -1.0, float(254 << 23), ALU.mult, ALU.add))
            two_e, two_me = ebits[:, 0:1].bitcast(F32), ebits[:, 1:2].bitcast(F32)
            for n, (src, f) in enumerate(((two_e, 2.0 ** -14), (two_e, 2.0 ** -13), (two_e, 2.0 ** -14 / 3),
                                          (two_me, H * 2.0 ** 14), (two_me, CLAMP * 2.0 ** 14),
                                          (two_me, -CLAMP * 2.0 ** 14), (two_me, (CLAMP - SHIFT) * 2.0 ** 14),
                                          (two_me, (-CLAMP - SHIFT) * 2.0 ** 14), (two_me, -SHIFT * 2.0 ** 14),
                                          (two_e, 2.0 ** -14 / H))):
                v.tensor_scalar(cs[:, n:n + 1], src, f, None, ALU.mult)
            link(v.tensor_scalar(pow2[:, 1:2], two_me, 2.0 ** 14, None, ALU.mult))
            v.tensor_copy(taps[:].rearrange("p k (c b) -> p k c b", b=B),
                          cols[:, :, 0:TAPS].rearrange("p c k -> p k c").unsqueeze(3).to_broadcast([P, TAPS, C, B]))
            link(v.tensor_scalar(neg_bias[:], cols[:, :, 9], -1.0, SHIFT, ALU.mult, ALU.add))
            link(v.tensor_tensor(cmaxb[:], cols[:, :, 8], neg_bias[:], ALU.subtract))
            v.tensor_copy(r8(conv_bias[:]), cmaxb[:].unsqueeze(2).to_broadcast([P, C, B]))
            v.tensor_copy(h_sigma[:], cs[:, 3:4].to_broadcast([P, CB])).then_inc(s_par, 1)
            v.memset(bounds[:, 0:1], BIG)
            v.memset(bounds[:, 1:2], -BIG)
            v.memset(bounds[:, 2:3], BIG)
            link(v.memset(bounds[:, 3:4], -BIG))
            link(v.tensor_scalar(r8(Z[0][:, 0:CB]), cols[:, :, 0:B], pow2[:, 1:2], None, ALU.mult))
            v.tensor_scalar(q3[:], Z[0][:, 0:CB], 3.0, None, ALU.mult)
            link(v.tensor_scalar(p3[:], Z[0][:, 0:CB], cs[:, 8:9], None, ALU.add))
            link(v.tensor_scalar(p3[:], p3[:], 3.0, None, ALU.mult))
            link(v.tensor_reduce(of_head[:], ident[:].rearrange("p (r j) -> p r j", j=DH), AX.X, ALU.add))
            link(v.tensor_scalar(gains[:, HPC:HPC + 1], cols[:, 0, 14:15], SCALE3, None, ALU.mult))
            link(v.tensor_scalar(gains[:, 0:HPC], of_head[:], cols[:, 0, 13:14], None, ALU.mult))
            v.tensor_reduce(fold[:], ident[:].rearrange("p (a j) -> p j a", j=DK), AX.X, ALU.add).then_inc(s_fold, 1)
            with dve.Fori(0, B // 2) as i:
                for j in (0, 2):
                    dve.wait_ge(s_xt, i * 4 + (j + 2))
                    bb, tc = i * 2 + j // 2, j % 2
                    dst = padded[:, (TAPS - 1 + tc * P) * CB:(TAPS - 1 + (tc + 1) * P) * CB] \
                        .rearrange("p (t c b) -> p b c t", c=C, b=B)
                    v.tensor_copy(dst[:, bass.ds(bb, 1)].rearrange("p o c t -> p (o c) t"),
                                  bank[j][:].rearrange("p (c t) -> p c t", c=C)).then_inc(s_xe[0], 1)
            for mc in range(C):
                dve.wait_ge(s_ct, mc + 1)
                link(v.tensor_scalar(coup_t[:, mc], bank[mc][:], H, pow2[:, 1:2], ALU.mult, ALU.mult))
                link(v.tensor_copy(c_hi[:, mc], coup_t[:, mc]))
                ins = v.tensor_tensor(c_lo[:, mc], coup_t[:, mc], c_hi[:, mc], ALU.subtract)
            ins.then_inc(s_chi, 1)
            dve.wait_ge(s_emb, 1)
            emb = bank[4][:, 64:64 + 2 * CB].rearrange("p (n b) -> p n b", b=B)
            pr = params[:].rearrange("p b n -> p n b")
            v.tensor_copy(pr[:, 0:4], cols[:, :, 0:B])
            bc = lambda r: cols[:, :, r:r + 1].to_broadcast([P, C, B])
            v.tensor_tensor(pr[:, 8:12], emb[:, 4:8], bc(12), ALU.add)
            link(v.tensor_tensor(pr[:, 4:8], emb[:, 0:4], bc(11), ALU.add))
            link(v.tensor_scalar(pr[:, 4:8], pr[:, 4:8], 1.0, None, ALU.add))
            v.tensor_tensor(pr[:, 4:8], pr[:, 4:8], bc(10), ALU.mult).then_inc(s_prm, 1)
            dve.wait_ge(s_prm, 1)
            dve.wait_ge(s_ld, 16 * 7)
            v.tensor_reduce(vmax[:, 0:1], params[:, :, 4:12], AX.XY, ALU.max,
                            apply_absolute_value=True)
            link(v.tensor_reduce(wvmax[:], wqkv[:, :, 2 * D:3 * D], AX.X, ALU.max, apply_absolute_value=True))
            v.tensor_reduce(vmax[:, 1:2], wvmax[:], AX.X, ALU.max).then_inc(s_vm, 1)
            dve.wait_ge(s_wos, 1)
            link(v.tensor_copy(wo_sum[:], bank[7][0:DK, 0:T]))
            v.tensor_scalar(q3[:], Z[0][:, 0:CB], 3.0, None, ALU.mult).then_inc(s_chi, 1)
            v.tensor_scalar(cs[:, 9:10], two_e, 2.0 ** -14 / H, None, ALU.mult).then_inc(s_const, 1)
            dve.wait_ge(s_chi, 2)
            dve.wait_ge(s_const, 1)
            v.tensor_copy(yv[:], q3[:]).then_inc(s_q[0], 1)

            def reduced(k, step):
                dve.wait_ge(s_b[k], step)
                dve.wait_ge(s_mm[k], step)
                v.tensor_reduce((Z[1][:, 0:CB], Z[2][:, 0:CB], q4h[:], q3[:])[k], psS.rearrange("p s c -> p c s"),
                                AX.X, ALU.add).then_inc(s_q[(k + 1) % 4], 1)

            def clip_q(step):
                v.tensor_scalar(p3[:], p3[:], 1.0 / 3.0, bounds[:, 2:3], ALU.mult, ALU.min).then_inc(s_pv, 1)
                dve.wait_ge(s_q[0], step)
                v.tensor_scalar(qv[:], q3[:], 1.0 / 3.0, bounds[:, 0:1], ALU.mult, ALU.min).then_inc(s_qv, 1)
                dve.wait_ge(s_qv, step)
                v.tensor_scalar(Z[0][:, 0:CB], qv[:], bounds[:, 1:2], None, ALU.max).then_inc(s_clip, 1)

            def addend(k, step, dr):
                q, p = Z[k][:, 0:CB], Z[k][:, CB:2 * CB]
                if k in (1, 2):
                    dve.wait_ge(s_q[k], step)
                    STT(yv[:], p, -BETA, q, ALU.mult, ALU.add).then_inc(s_y[k], 1)
                    if k == 1:
                        v.tensor_tensor(acc[:], Z[1][:], Z[0][:], ALU.subtract)
                    else:
                        STT(acc[:], Z[2][:], 2.0, acc[:], ALU.mult, ALU.add).then_inc(s_acc, 1)
                if k == 3:
                    dve.wait_ge(s_q[3], step)
                    dve.wait_ge(s_accd, step)
                    STT(acc_hd[:], q4h[:], 2.0, acc_d[:], ALU.mult, ALU.add).then_inc(s_hd[3], 1)
                    STT(yv[:], q4h[:], 2.0, beta_p[:], ALU.mult, ALU.add).then_inc(s_y[3], 1)
                dve.wait_ge(s_tf[k], step)
                v.tensor_tensor(tanh_hl[:, :, B:2 * B], r8(tanh_f[:]), tanh_hl[:, :, 0:B],
                                ALU.subtract).then_inc(s_lo[k], 1)
                if k == 0:
                    dve.wait_ge(s_pv, step)
                    v.tensor_scalar(Z[0][:, CB:2 * CB], p3[:], bounds[:, 3:4], None, ALU.max).then_inc(s_p0, 1)
                    dve.wait_ge(s_clip, step)
                    dve.wait_ge(s_drv, step)
                    v.tensor_tensor(q_hd[:], dr, q, ALU.add).then_inc(s_hd[0], 1)
                    dve.wait_ge(s_p0, step)
                    STT(yv[:], p, -BETA, q, ALU.mult, ALU.add).then_inc(s_y[0], 1)
                dve.wait_ge(s_sq[k], step)
                STT(cub[:], qsq[:], 3.0, q if k < 3 else q4h[:], ALU.subtract, ALU.mult)
                if k == 0:
                    dve.wait_ge(s_hd[0], step)
                if k == 3:
                    dve.wait_ge(s_hd[3], step)
                STT(wv_[:], p, -H, (q_hd, q_hd, q_hd2, acc_hd)[k][:], ALU.mult, ALU.add).then_inc(s_w[k], 1)
                dve.wait_ge(s_y[k], step)
                if k < 3:
                    STT(Z[k + 1][:, CB:2 * CB], yv[:], (1, 1, 2)[k] * H * EPSILON, Z[0][:, CB:2 * CB],
                        ALU.mult, ALU.add).then_inc(s_p[k + 1], 1)
                else:
                    STT(p3[:], yv[:], H * EPSILON, acc[:, CB:2 * CB], ALU.mult, ALU.add)
                dve.wait_ge(s_w[k], step)
                STT(psC[:, 2, 0:CB], cub[:], -(1, 1, 1, 2)[k] * H / 3, wv_[:], ALU.mult,
                    ALU.add).then_inc(s_b[k], 1)
                if k == 0:
                    STT(q_hd2[:], q, 0.5, dr, ALU.mult, ALU.add)
                if k == 1:
                    v.tensor_copy(bounds[:], cs[:, 4:8])
                if k == 2:
                    dve.wait_ge(s_p[3], step)
                    v.tensor_scalar(beta_p[:], Z[3][:, CB:2 * CB], -BETA, None, ALU.mult)
                    dve.wait_ge(s_acc, step)
                    v.tensor_tensor(acc_d[:], dr, acc[:, 0:CB], ALU.add)
                    v.tensor_tensor(acc[:, CB:2 * CB], Z[3][:, CB:2 * CB], acc[:, CB:2 * CB],
                                    ALU.add).then_inc(s_accd, 1)

            def stages(step, dr):
                clip_q(step)
                for k in range(3):
                    addend(k, step, dr)
                    reduced(k, step)
                addend(3, step, dr)

            stages(1, drive[:, 0])
            with dve.Fori(0, T - 1) as t:
                step = dve.snap(t + 1)
                after = dve.snap(t + 2)
                reduced(3, step)
                stages(after, drive[:, bass.ds(t + 1, 1), :].rearrange("p o c -> p (o c)"))
            reduced(3, T)
            clip_q(T + 1)
            dve.wait_ge(s_vma, 2)
            link(v.tensor_scalar(vscale[:, 1:2], vmax[:, 2:3], (D ** 0.5 + 1) * 1.01 * D, vmax[:, 3:4], ALU.mult,
                                 ALU.mult))
            link(v.tensor_scalar(vscale[:, 1:2], vscale[:, 1:2], 2.0 ** -100, 2.0 ** 100, ALU.max, ALU.min))
            link(v.tensor_scalar(vbits[:, 0:1], vscale[:, 1:2].bitcast(I32), 0x7F800000, None, ALU.bitwise_and))
            link(v.tensor_scalar(vbits[:, 1:2], vbits[:, 0:1], -1.0, float(254 << 23), ALU.mult, ALU.add))
            v.tensor_scalar(vscale[:, 0:1], vbits[:, 1:2].bitcast(F32), 2.0 ** 14, None,
                            ALU.mult).then_inc(s_vs, 1)
            dve.wait_ge(s_vs, 1)
            dve.wait_ge(s_tr, 1)
            tr3 = trace[:, CB:(T + 1) * CB].rearrange("p (t c b) -> p b c t", c=C, b=B)
            dr3 = drive[:].rearrange("p t (c b) -> p b c t", b=B)
            with dve.Fori(0, B) as b:
                S["hm"].wait(dve, b, 32)
                S["hm_done"].by(v.tensor_scalar(k2t[32:33, :], k2t[32:33, :], -1.0, 1.0, ALU.mult, ALU.add))
                S["hm_done"].wait(dve, b, 1)
                S["hm_done"].by(v.tensor_scalar(k2t[32:33, :], k2t[32:33, :], -1e30, None, ALU.mult))
                S["xtr"].wait(dve, b, 0)
                for c in range(C):
                    S["x2t"].by(v.tensor_scalar(x1t[:, c], dr3[:, bass.ds(b, 1), c].rearrange("p o t -> p (o t)"),
                                                cs[:, 9:10], neg_bias[:, c:c + 1], ALU.mult, ALU.add))
                S["x2t"].wait(dve, b, 4)
                S["x2t"].by(STT(x2t, tr3[:, bass.ds(b, 1)].rearrange("p o c t -> p (o c) t"), cs[:, 0:1], x1t,
                                ALU.mult, ALU.add))
                S["xtr"].wait(dve, b, 2)
                S["x2"].by(v.tensor_copy(x2[:, 1], bank[1][:]))
                S["proj"].wait(dve, b, 1)
                S["qkv2"].wait(dve, b, 1)
                S["hm"].wait(dve, b, 32)
                S["kk"].by(v.tensor_tensor(k2t[0:DK, :], bank[2][32:32 + DK, :], hmask[:], ALU.mult))
                for qc in range(C):
                    S["sc"].wait(dve, b, qc + 1)
                    S["mx"].by(v.tensor_reduce(negmax2[:, qc:qc + 1], bank[qc % 2][:], AX.X, ALU.max, negate=True))
                S["pv"].wait(dve, b, 1)
                O = bank[3][:, 128:128 + C * 17].rearrange("p (c k) -> p c k", k=17)
                S["h2"].by(v.reciprocal(rden2[:], O[:, :, DK]))
                S["par"].wait(dve, b, 1)
                S["h2"].wait(dve, b, 1)
                S["h2"].by(v.tensor_tensor(rmask2[:], rden2[:], par[:, 0:C], ALU.mult))
                S["h2"].wait(dve, b, 2)
                S["h2"].by(v.tensor_tensor(head2[:], O[:, :, 0:DK], rmask2[:].unsqueeze(2).to_broadcast([P, C, DK]),
                                           ALU.mult))
                for tc in range(TC):
                    S["o2"].wait(dve, b, tc + 1)
                    S["x3"].by(v.tensor_tensor(x3[:, tc], bank[tc][:], x2[:, tc], ALU.add))
                S["ss"].wait(dve, b, 2)
                S["ms"].by(v.tensor_scalar(ms3[:], ss3[:], 1.0 / D, RMS_EPS, ALU.mult, ALU.add))
                S["r3"].wait(dve, b, 1)
                S["xnp"].wait(dve, b, 0)
                for tc in range(TC):
                    S["x3n"].by(v.tensor_scalar(x3n[:, tc], x3[:, tc], r3[:, tc:tc + 1], None, ALU.mult))

                def head_queries(tc):
                    S["qkt"].wait(dve, b, 3 * tc + 2)
                    for r in (2, 3):
                        S["qkt2"].by(v.tensor_scalar(qth[r][:, :, tc * P:(tc + 1) * P],
                                                     bank[6][:].rearrange("p (c t) -> p c t", c=C),
                                                     gains[:, r:r + 1], None, ALU.mult))

                for i in range(4):
                    tc, j = i // 2, i % 2
                    m = tc * 3 + j
                    S["sqr"].wait(dve, b, i + 1)
                    S["hs"].by(v.tensor_reduce(hss[:, i], sqs[i % 2][:].rearrange("p (h d) -> p h d", d=DH), AX.X, ALU.add))
                    S["hs"].wait(dve, b, i + 1)
                    S["hm3"].by(v.tensor_scalar(hms[:, i], hss[:, i], 1.0 / DH, RMS_EPS, ALU.mult, ALU.add))
                    S["hr"].wait(dve, b, i + 1)
                    if i >= 2:
                        S["qkp"].wait(dve, b, i - 1)
                    S["qkn"].by(v.tensor_tensor(qkn[i % 2][:].rearrange("p (h d) -> p h d", d=DH),
                                                bank[m][:].rearrange("p (h d) -> p h d", d=DH),
                                                hr[:, i].unsqueeze(2).to_broadcast([P, NH, DH]), ALU.mult))
                    if i == 2:
                        head_queries(0)
                    if j == 1:
                        S["v3"].wait(dve, b, tc + 1)
                        S["v3l"].by(STT(v3l[:, tc], bank[tc * 3 + 2][:], vscale[:, 0:1], v3h[:, tc], ALU.mult,
                                        ALU.subtract))

                head_queries(1)

                def maxima(h):
                    S["s3"].wait(dve, b, h + 1)
                    S["m3"].by(v.tensor_reduce(negmax3[:, h % 2], bank[h % 2][:].rearrange("p (q k) -> p q k", k=T),
                                               AX.X, ALU.max, negate=True))

                maxima(0)
                maxima(1)
                for h in range(NH):
                    if h + 2 < NH:
                        maxima(h + 2)
                    S["eth"].wait(dve, b, h + 1)
                    if h >= 2:
                        S["pv3"].wait(dve, b, h - 1)
                    S["etl"].by(v.tensor_tensor(e3t_lo[h % 2][:].rearrange("p k t -> p (k t)"), bank[2 + h % 2][:],
                                                e3t_hi[h % 2][:].rearrange("p k t -> p (k t)"), ALU.subtract))
                S["e3"].wait(dve, b, NH)
                S["rd"].by(v.tensor_scalar(den3[:], den3[:], vscale[:, 0:1], None, ALU.mult))
                S["rd"].wait(dve, b, 1)
                S["rd"].by(v.reciprocal(rden3[:], den3[:]))
                S["rd"].wait(dve, b, 2)
                S["pv3"].wait(dve, b, NH)
                for tc in range(TC):
                    S["on"].by(v.tensor_tensor(o_sb[:, tc].rearrange("p (h d) -> p h d", d=DH),
                                               bank[4 + tc][:].rearrange("p (h d) -> p h d", d=DH),
                                               rden3[:, tc].unsqueeze(2).to_broadcast([P, NH, DH]), ALU.mult))
                S["on"].wait(dve, b, 2)
                S["stored"].wait(dve, b, 0)
                for tc in range(TC):
                    S["rs"].by(v.tensor_tensor(res[:, tc], o_sb[:, tc], x3[:, tc], ALU.add))
                for tc in range(TC):
                    S["rs"].wait(dve, b, tc + 1)
                    S["op"].wait(dve, b, tc + 1)
                    S["res"].by(v.tensor_tensor(res[:, tc], bank[6 + tc][:], res[:, tc], ALU.add))

        for name, signal_ in S.items():
            assert name in ("hm", "stored") or signal_.n == signal_.per, name


_INS = ["x", "cond_2048", "L0_cond_b", "L1_cond_coupling", "L1_cond_bias", "L2_cond_Wq", "L2_cond_Wk", "L2_cond_Wv",
        "L2_cond_Wo", "L3_cond_W_emb", "L3_cond_b_emb", "L3_cond_g_norm", "L3_cond_W_qkv", "L3_cond_g_q",
        "L3_cond_g_k", "L3_cond_W_out"]


def kernel(**inputs):
    import numpy as np
    import concourse.bacc as bacc
    from concourse import mybir
    from concourse.bass_utils import run_bass_kernel_spmd

    nc = bacc.Bacc("TRN2", target_bir_lowering=False, num_devices=1)
    arrays, args = {}, []
    for name in _INS:
        a = np.ascontiguousarray(inputs[name])
        arrays[f"in_{name}"] = a
        args.append(nc.dram_tensor(f"in_{name}", a.shape, mybir.dt.from_np(a.dtype), kind="ExternalInput").ap())
    args.append(nc.dram_tensor("out", inputs["x"].shape, mybir.dt.float32, kind="ExternalOutput").ap())
    build(nc, *args)
    r = run_bass_kernel_spmd(nc, [arrays], core_ids=[0])
    return r.results[0]["out"]
```

```python
from contextlib import ExitStack

import concourse.bass as bass
from concourse import mybir

F32 = mybir.dt.float32
F16 = mybir.dt.float16
I32 = mybir.dt.int32
ALU = mybir.AluOpType
ACT = mybir.ActivationFunctionType
AX = mybir.AxisListType
RMAX = bass.bass_isa.ReduceOp.max

P = 128
DT = 0.01
H = DT / 2
EPSILON, ALPHA, BETA, CLAMP = 0.08, 0.7, 0.8, 20.0
SHIFT = ALPHA / BETA
RMS_EPS = 1e-6
BIG = 3.0e38


class Signal:

    def __init__(self, sem, per, base=0):
        self.sem, self.per, self.base, self.n = sem, per, base, 0

    def by(self, ins):
        self.n += 1
        ins.then_inc(self.sem, 1)
        return self.n

    def wait(self, eng, turn, n):
        eng.wait_ge(self.sem, turn * self.per + (self.base + n))



def build(nc, x, cond, L0_b, coupling, L1_bias, Wq, Wk, Wv, Wo, W_emb, b_emb, g_norm, W_qkv, g_q, g_k,
          W_out, out):
    B, T, D = x.shape
    TAPS = cond.shape[0]
    C = D // P
    TC = T // P
    CB = C * B
    HEADS, DK = Wq.shape[0], Wq.shape[2]
    DH = g_q.shape[0]
    NH = D // DH
    HPC = P // DH
    SCALE2 = float(DK) ** -0.5
    SCALE3 = float(DH) ** -0.5
    assert (B, C, TC, TAPS, DK, DH) == (8, 4, 2, 8, 16, 32)

    with ExitStack() as ctx:
        def sb(name, shape, dt=F32):
            return ctx.enter_context(nc.sbuf_tensor(name, shape, dt))

        def sem(name):
            return ctx.enter_context(nc.semaphore(name))

        padded = sb("padded_x", [P, (T + TAPS - 1) * CB])
        drive = sb("drive", [P, T, CB])
        trace = sb("trace", [P, (T + 1) * CB])
        c_hi = sb("c_hi", [P, C, D], F16)
        c_lo = sb("c_lo", [P, C, D], F16)
        wqkv = sb("wqkv", [P, C, 3 * D])
        wout = sb("wout", [P, C, D])
        ident = sb("ident", [P, P])
        coup = trace[:, 0:C * D].rearrange("p (c m) -> p c m", c=C)
        tiles = padded[:, 0:8 * TC * D].rearrange("p (i t d) -> p i t d", i=8, t=TC)
        wemb = tiles[:, 4:8].rearrange("p i t d -> p (i t d)").rearrange("p (c n) -> p c n", c=C)
        x2t = tiles[:, 0].rearrange("p t d -> p (t d)").rearrange("p (c t) -> p c t", c=C)
        x2, x3, x3n, o_sb, res, x3k = (tiles[:, i] for i in range(1, 7))
        o_t = tiles[:, 7].rearrange("p t d -> p (t d)").rearrange("p (c t) -> p c t", c=C)

        rows = sb("rows", [16, D])
        cols = sb("cols", [P, C, 16])
        taps = sb("taps", [P, TAPS, CB])
        conv_bias = sb("conv_bias", [P, CB])
        h_sigma = sb("h_sigma", [P, CB])
        neg_bias = sb("neg_bias", [P, C])
        cmax = sb("cmax", [P, 2])
        bias_diff = sb("bias_difference", [P, C])
        ebits = sb("ebits", [P, 2], I32)
        pow2 = sb("pow2", [P, 2])
        cs = sb("consts", [P, 10])
        q_upper = sb("upper_3q", [P, 1])
        q_lower = sb("lower_3q", [P, CB])
        p_upper = sb("p_upper", [P, CB])
        p_lower = sb("p_lower", [P, CB])
        gains = sb("gains", [P, HPC + 1])
        of_head = sb("of_head", [P, HPC])
        Z = [sb(f"stage{k}_qp", [P, 2 * CB]) for k in range(4)]
        tanh_hl = sb("tanh_hl", [P, C, 2 * B], F16)
        tanh_f = sb("tanh_f", [P, CB])
        qsq = sb("qsq", [P, CB])
        yv = sb("q_minus_beta_p", [P, CB])
        wv_ = sb("linear_part", [P, CB])
        cub = sb("cubic_part", [P, CB])
        q_hd = sb("q_plus_drive", [P, CB])
        q_hd2 = sb("half_q_plus_drive", [P, CB])
        acc_hd = sb("sum_but_slope_3", [P, CB])
        acc = sb("acc_qp", [P, 2 * CB])
        acc_d = sb("acc_plus_drive", [P, CB])
        sum3 = sb("qp_times_3", [P, 2 * CB])
        q3, p3 = sum3[:, 0:CB], sum3[:, CB:2 * CB]
        q0_3 = sb("stage0_3q", [P, CB])
        p_up = sb("p_bounded_above", [P, CB])
        p_kept = sb("p_less_its_slope", [P, CB])
        q4h = sb("stage3_half_q", [P, CB])
        prod = sb("prod", [P, TAPS * CB])
        half = sb("half_sum", [P, 4 * CB])
        quart = sb("quarter_sum", [P, 2 * CB])
        conv = sb("conv", [P, CB])
        xb = sb("x_plus_bias", [P, CB])
        dsum = sb("dsum", [P, CB])
        wqk2 = sb("wqk2", [P, TC, P])
        wv2 = sb("wv2", [P, TC, DK])
        wo2 = sb("wo2", [P, 2, T])
        fold = sb("fold", [P, DK])
        wo_sum = sb("wo_sum", [DK, T])
        params = sb("params", [P, B, 12])
        par = sb("par", [P, 12])
        hmask = sb("hmask", [DK, D])
        q2t = sb("q2t", [P, D])
        k2t = sb("k2t", [P, D])
        v2 = sb("v2", [P, C, DK + 1])
        negmax2 = sb("negmax2", [P, C])
        e2 = sb("e2", [P, C, D])
        rden2 = sb("rden2", [P, C])
        rmask2 = sb("rmask2", [P, C])
        head2 = sb("head2", [P, C, DK])
        head2t = sb("head2t", [DK, D])
        ss3 = sb("ss3", [P, TC])
        ms3 = sb("ms3", [P, TC])
        r3 = sb("r3", [P, TC])
        xnt = sb("xnt", [P, C, T])
        sqs = [sb(f"sq_{i}", [P, D]) for i in range(2)]
        hss = sb("head_ss", [P, 4, NH])
        hms = sb("head_ms", [P, 4, NH])
        hr = sb("head_r", [P, 4, NH])
        halves = sb("minus_half", [P, NH])
        ones = sb("ones", [P, 1])
        factors = sb("factors", [P, 2])
        qkn = [sb(f"qkn_{i}", [P, D]) for i in range(2)]
        qth = [c_.rearrange("p c m -> p (c m)").bitcast(F32).rearrange("p (c t) -> p c t", c=C)
               for c_ in (c_hi[:], c_lo[:])] + [sb(f"qt_{i}", [P, C, T]) for i in (2, 3)]
        kt = sb("kt", [P, C, T])
        v3h = sb("v3_hi", [P, TC, D], F16)
        v3l = sb("v3_lo", [P, TC, D], F16)
        vmax = sb("v_bound_parts", [P, 4])
        wvmax = sb("wv_max", [P, C])
        vbits = sb("v_exponent", [P, 2], I32)
        vscale = sb("v_scale", [P, 2])
        negmax3 = sb("negmax3", [P, 2, TC])
        e3 = [sb(f"e3_{i}", [P, TC, T]) for i in range(2)]
        e3t_hi = [sb(f"e3t_hi_{i}", [P, TC, T], F16) for i in range(2)]
        e3t_lo = [sb(f"e3t_lo_{i}", [P, TC, T], F16) for i in range(2)]
        den3 = sb("den3", [P, TC, NH])
        rden3 = sb("rden3", [P, TC, NH])
        xl = [e2[:, j] for j in range(4)]

        bank = [ctx.enter_context(nc.psum_tensor(f"bank{i}", [P, 512], F32)) for i in range(5)]
        psC = ctx.enter_context(nc.psum_tensor("psC", [P, 6, 256], F32))
        bank += [psC[:, 2 * i:2 * i + 2, :].rearrange("p a b -> p (a b)") for i in range(3)]
        HALF = CB // 2
        CH = C // 2
        ps_half = [psC[:, 0:3, 0:HALF], psC[:, 3:6, 0:HALF]]
        ps_prod = [psC[:, 0:2, 0:HALF], psC[:, 4:6, 0:HALF]]

        s_ld = sem("weights_loaded")
        s_lc = sem("coupling_loaded")
        s_lr = sem("rows_loaded")
        s_rowz = sem("rows_cleared")
        s_id = sem("identity_ready")
        s_pool = sem("pool_chain")
        s_colp = sem("cols_transposed")
        s_cols = sem("cols_ready")
        s_cm = sem("coupling_max")
        s_cma = sem("coupling_max_all")
        s_ct = sem("coupling_transposed")
        s_vec0 = sem("vector_chain_prep")
        s_par = sem("conv_params_ready")
        s_const = sem("consts_ready")
        s_hic = sem("coupling_hi_ready")
        s_chi = sem("state_and_coupling_ready")
        s_emb = sem("emb_products")
        s_prm = sem("params_ready")
        s_fold = sem("fold_ready")
        s_wos = sem("wo_products")
        s_xl = [sem(f"x_loaded{j}") for j in range(4)]
        s_xt = sem("x_transposed")
        s_xe = [sem(f"x_evacuated{j}") for j in range(2)]
        s_pad = sem("pad_cleared")
        s_drv = sem("drive_ready")
        s_q, s_hi, s_tf, s_lo, s_mm = ([[sem(f"stage{k}_{name}_half{x}") for x in range(2)] for k in range(4)]
                                       for name in ("q", "tanh_hi", "tanh_f", "tanh_lo", "coupling"))
        s_sq = [sem(f"stage{k}_q_squared") for k in range(4)]
        s_clip = sem("q_clipped")
        s_p3 = sem("p3_ready")
        s_up = sem("p_bounded_above")
        s_p0 = sem("stage0_p")
        s_p = [None] + [sem(f"stage{k}_p") for k in range(1, 4)]
        s_y = [sem(name) for name in ("stage0_p_less_its_slope", "stage1_y", "stage2_y")]
        s_acc = [None, sem("stage1_acc"), sem("stage2_acc")]
        s_accd = sem("acc_plus_drive")
        s_accp = sem("acc_p_ready")
        s_hd = [sem("stage0_q_plus_drive"), None, None, sem("stage3_acc_plus_slope")]
        s_hd2 = sem("half_q_plus_drive")
        s_w = [sem(f"stage{k}_linear") for k in range(4)]
        s_b = [sem(f"stage{k}_addend") for k in range(4)]
        s_tr = sem("trace_done")
        s_vm = sem("v_bound_parts_ready")
        s_vs = sem("v_scale_ready")
        s_vma = sem("v_bound_parts_all")

        block = ctx.enter_context(nc.Block())

        def r8(a):
            return a.rearrange("p (c b) -> p c b", b=B)

        def signal(name, per):
            return Signal(sem(name), per, 1)

        def tail_signals():
            return dict(
                hm=signal("hmask_loaded", 32), hm_done=signal("mask_row_ready", 2),
                par=signal("batch_params", 1),
                x2t=signal("x2t_ready", 4), xtr=signal("x2_transposed", 2), x2=signal("x2_ready", 2),
                proj=signal("l2_proj", 2), qkv2=signal("l2_qkv_ready", 2),
                kk=signal("l2_keys_ready", 1), sc=signal("l2_scores", 4), mx=signal("l2_max", 4),
                mt=signal("l2_max_row", 1),
                mrow=signal("l2_max_ready", 1), st=signal("l2_scores_t", 4), e2=signal("l2_exp", 4),
                pv=signal("l2_pv", 1), h2=signal("l2_head", 3), h2t=signal("l2_head_t", 1),
                h2e=signal("l2_head_t_ready", 1), o2=signal("l2_out", 2), x3=signal("x3_ready", 2),
                ss=signal("x3_squares", 2), ms=signal("x3_mean", 1), r3=signal("x3_rms", 1),
                x3n=signal("x3_normed", 2), xnp=signal("xn_transposed", 2), xnt=signal("xnt_ready", 4),
                keep=signal("x3_kept", 1),
                qkv=signal("l3_qkv", 6), sqr=signal("qk_squares", 4), hs=signal("qk_sums", 4),
                hm3=signal("qk_means", 4), hr=signal("qk_rms", 4), qkn=signal("qk_normed", 4),
                v3=signal("v3_hi_ready", 2), v3l=signal("v3_lo_ready", 2), qkp=signal("qk_transposed", 4),
                qkt=signal("qkt_ready", 6), qkt2=signal("qkt_ready_too", 4),
                s3=signal("l3_scores", NH), m3=signal("l3_max", NH), e3=signal("l3_exp", NH),
                et=signal("l3_probs_t", NH), eth=signal("l3_probs_t_hi", NH), etl=signal("l3_probs_t_lo", NH),
                pv3=signal("l3_pv", NH),
                rd=signal("l3_rden", 2), on=signal("l3_o_ready", 2), ot=signal("l3_o_t", 2),
                ote=signal("l3_o_t_ready", 2), op=signal("l3_out", 2), rs=signal("res_part", 2),
                res=signal("res_ready", 2), stored=signal("stored", 32))

        S = tail_signals()

        MAX_ROW, KEY_SCORES, WEIGHTED, HEAD_TURNED, L2_OUT, NORMED = 0, (1, 3), (5, 6), 8, 9, 14

        @block.sync
        def _(sp):
            sp.sem_inc(s_xt, 4)
            for signal_ in (*s_xe, *(one_.sem for one_ in S.values())):
                sp.sem_inc(signal_, 1)
            sp.dma_start(coup, coupling.rearrange("(c p) m -> p c m", p=P)).then_inc(s_lc, 16)
            one = lambda a: a.rearrange("(o d) -> o d", o=1)
            sp.dma_start(rows[0:B, :], cond).then_inc(s_lr, 16)
            for r, v in ((8, one(L0_b)), (9, one(L1_bias)), (10, one(g_norm)), (11, one(b_emb[0:D])),
                         (12, one(b_emb[D:2 * D])), (15, one(L0_b))):
                sp.dma_start(rows[r:r + 1, :], v).then_inc(s_lr, 16)
            for r, v in ((13, g_q), (14, g_k)):
                sp.dma_start(rows[r:r + 1, :].rearrange("o (h d) -> o h d", d=DH),
                             one(v).unsqueeze(1).to_broadcast([1, NH, DH])).then_inc(s_lr, 16)
            with sp.Fori(0, B // 2) as i:
                for j in range(4):
                    sp.wait_ge(s_xt, i * 4 + (j + 1))
                    sp.dma_start(xl[j], x[bass.ds(i * 2 + j // 2, 1), (j % 2) * P:(j % 2 + 1) * P, :]
                                 .rearrange("o t d -> (o t) d")).then_inc(s_xl[j], 16)
            sp.wait_ge(s_rowz, 1)
            sp.dma_start(wqk2[:, :, 0:DK], Wq[1].rearrange("(c p) k -> p c k", p=P)).then_inc(s_ld, 16)
            sp.dma_start(wqk2[:, :, 32:32 + DK], Wk[1].rearrange("(c p) k -> p c k", p=P)).then_inc(s_ld, 16)
            sp.dma_start(wv2[:], Wv[1].rearrange("(c p) k -> p c k", p=P)).then_inc(s_ld, 16)
            sp.dma_start(wo2[:], Wo.rearrange("(c p) t -> p c t", p=P)).then_inc(s_ld, 16)
            sp.dma_start(wqkv[:], W_qkv.rearrange("(c p) n -> p c n", p=P)).then_inc(s_ld, 16)
            sp.dma_start(wout[:], W_out.rearrange("(c p) n -> p c n", p=P)).then_inc(s_ld, 16)
            sp.wait_ge(s_drv, T)
            sp.dma_start(wemb, W_emb.rearrange("(c p) n -> p c n", p=P)).then_inc(s_ld, 16)

            def masks(f):
                S["st"].wait(sp, f, 0)
                row = cond[bass.ds(f, 1), :]
                sp.dma_start(hmask[:], row.to_broadcast([DK, D])).then_inc(S["hm"].sem, 16)
                sp.dma_start(k2t[32:33, :], row).then_inc(S["hm"].sem, 16)

            def store(b):
                for tc in range(TC):
                    S["res"].wait(sp, b, tc + 1)
                    sp.dma_start(out[bass.ds(b, 1), tc * P:(tc + 1) * P, :].rearrange("o t d -> (o t) d"),
                                 res[:, tc]).then_inc(S["stored"].sem, 16)

            masks(0)
            masks(1)
            with sp.Fori(0, B - 2) as b:
                masks(b + 2)
                store(b)
            store(B - 2)
            store(B - 1)
            sp.wait_ge(S["stored"].sem, 32 * B + 1)

        @block.gpsimd
        def _(pool):
            g = nc.gpsimd
            g.memset(ident[:], 0.0).then_inc(s_pool, 1)
            pool.wait_ge(s_pool, 1)
            g.affine_select(out=ident[:], in_=ident[:], compare_op=ALU.not_equal, fill=1.0, base=0,
                            pattern=[[-1, P]], channel_multiplier=1).then_inc(s_id, 1)
            g.memset(wqk2[:], 0.0).then_inc(s_rowz, 1)
            g.memset(padded[:, 0:(TAPS - 1) * CB], 0.0).then_inc(s_pad, 1)
            g.memset(halves[:], -0.5)
            g.memset(ones[:], 1.0)
            g.memset(factors[:, 0:1], 1.0 / H)
            g.memset(factors[:, 1:2], -1e30)
            g.memset(q2t[:], 0.0)
            g.memset(k2t[:], 0.0)
            g.memset(v2[:], 1.0).then_inc(s_pool, 1)
            pool.wait_ge(s_pool, 2)
            g.memset(q2t[32:33, :], 1.0)
            g.memset(k2t[64:65, :], 1.0).then_inc(s_pool, 1)
            pool.wait_ge(s_pool, 3)
            pool.wait_ge(s_cm, 1)
            g.partition_all_reduce(cmax[:, 1:2], cmax[:, 0:1], P, RMAX).then_inc(s_cma, 1)
            pool.wait_ge(s_par, 1)
            pool.wait_ge(s_pool, 3)
            pool.wait_ge(s_pad, 1)
            for e in s_xe:
                pool.wait_ge(e, B + 1)
            ch = Signal(s_pool, 6, 3)
            with pool.Fori(0, T) as t:
                ch.wait(pool, t, 0)
                win = padded[:, bass.ds(t * CB, TAPS * CB)]
                g.tensor_tensor(prod[:], win, taps[:].rearrange("p k c -> p (k c)"), ALU.mult).then_inc(s_pool, 1)
                g.tensor_tensor(xb[:], padded[:, bass.ds(t * CB + (TAPS - 1) * CB, CB)], conv_bias[:],
                                ALU.add).then_inc(s_pool, 1)
                ch.wait(pool, t, 2)
                g.tensor_tensor(half[:], prod[:, 0:4 * CB], prod[:, 4 * CB:8 * CB], ALU.add).then_inc(s_pool, 1)
                ch.wait(pool, t, 3)
                g.tensor_tensor(quart[:], half[:, 0:2 * CB], half[:, 2 * CB:4 * CB], ALU.add).then_inc(s_pool, 1)
                ch.wait(pool, t, 4)
                g.tensor_tensor(conv[:], quart[:, 0:CB], quart[:, CB:2 * CB], ALU.add).then_inc(s_pool, 1)
                ch.wait(pool, t, 5)
                g.tensor_tensor(dsum[:], conv[:], xb[:], ALU.add).then_inc(s_pool, 1)
                ch.wait(pool, t, 6)
                g.tensor_tensor(drive[:, bass.ds(t, 1), :].rearrange("p o c -> p (o c)"), dsum[:], h_sigma[:],
                                ALU.mult).then_inc(s_drv, 1)
            pool.wait_ge(s_drv, T)
            pool.wait_ge(s_tr, 1)
            tr3 = trace[:, CB:(T + 1) * CB].rearrange("p (t c b) -> p b c t", c=C, b=B)
            dr3 = drive[:].rearrange("p t (c b) -> p b c t", b=B)

            def x2_features(f):
                S["r3"].wait(pool, f, 0)
                S["hm"].wait(pool, f, 32)
                row = k2t[32:33, :]
                S["hm_done"].by(g.tensor_tensor(row, ones[32:33, :].to_broadcast([1, D]), row, ALU.subtract))
                S["hm_done"].wait(pool, f, 1)
                S["hm_done"].by(g.tensor_tensor(row, row, factors[32:33, 1:2].to_broadcast([1, D]), ALU.mult))
                S["hm_done"].wait(pool, f, 2)
                S["xtr"].wait(pool, f, 0)
                flat = x2t.rearrange("p c t -> p (c t)")
                S["x2t"].by(g.tensor_tensor(x2t, dr3[:, bass.ds(f, 1)].rearrange("p o c t -> p (o c) t"),
                                            factors[:, 0:1].unsqueeze(2).to_broadcast([P, C, T]), ALU.mult))
                S["x2t"].wait(pool, f, 1)
                S["x2t"].by(g.tensor_tensor(x2t, tr3[:, bass.ds(f, 1)].rearrange("p o c t -> p (o c) t"), x2t, ALU.add))
                S["x2t"].wait(pool, f, 2)
                S["x2t"].by(g.tensor_tensor(flat, flat, cs[:, 0:1].to_broadcast([P, C * T]), ALU.mult))
                S["x2t"].wait(pool, f, 3)
                S["x2t"].by(g.tensor_tensor(x2t, x2t, neg_bias[:].unsqueeze(2).to_broadcast([P, C, T]), ALU.add))

            x2_features(0)
            pool.wait_ge(s_prm, 1)
            pool.wait_ge(s_vm, 1)
            for i in range(2):
                g.partition_all_reduce(vmax[:, 2 + i:3 + i], vmax[:, i:i + 1], P, RMAX).then_inc(s_vma, 1)

            def batch_params(f):
                S["xnt"].wait(pool, f, 0)
                S["h2"].wait(pool, f, 0)
                S["par"].by(g.tensor_copy(par[:], params[:, bass.ds(f, 1), :].rearrange("p o c -> p (o c)")))

            def x3_rms(f):
                S["ms"].wait(pool, f, 1)
                S["r3"].by(g.tensor_tensor(r3[:], ms3[:], halves[:, 0:TC], ALU.pow))

            def back(b):
                S["x3"].wait(pool, b, 2)
                S["rs"].wait(pool, b, 0)
                S["keep"].by(g.tensor_tensor(x3k, x3, ones[:].unsqueeze(2).to_broadcast([P, TC, D]), ALU.mult))
                for i in range(4):
                    S["hm3"].wait(pool, b, i + 1)
                    S["hr"].by(g.tensor_tensor(hr[:, i], hms[:, i], halves[:], ALU.pow))

            batch_params(0)
            x3_rms(0)
            with pool.Fori(0, B - 1) as b:
                x2_features(b + 1)
                back(b)
                batch_params(b + 1)
                x3_rms(b + 1)
            back(B - 1)

        @block.scalar
        def _(act):
            a = nc.scalar
            with act.Fori(0, B // 2) as i:
                for j in (1, 3):
                    act.wait_ge(s_xt, i * 4 + (j + 5))
                    bb, tc = i * 2 + j // 2, j % 2
                    dst = padded[:, (TAPS - 1 + tc * P) * CB:(TAPS - 1 + (tc + 1) * P) * CB] \
                        .rearrange("p (t c b) -> p b c t", c=C, b=B)
                    a.copy(dst[:, bass.ds(bb, 1)].rearrange("p o c t -> p (o c) t"),
                           bank[j][:].rearrange("p (c t) -> p c t", c=C)).then_inc(s_xe[1], 1)
            act.wait_ge(s_par, 1)
            for mc in range(C):
                act.wait_ge(s_ct, mc + 1)
                a.activation(c_hi[:, mc], bank[mc][:], ACT.Copy, scale=cs[:, 3:4]).then_inc(s_hic, 1)
            a.preload_act_table(ACT.Tanh)
            act.wait_ge(s_const, 1)
            scale = []
            for j in range(3):
                reg = act.alloc_register(f"tanh_scale{j}")
                act.reg_load(reg, cs[0:1, j:j + 1].bitcast(I32))
                scale.append(reg)
            with act.Fori(0, T) as t:
                step = act.snap(t + 1)
                for k in range(4):
                    src, s = ((q3, scale[2]), (Z[1][:, 0:CB], scale[0]), (Z[2][:, 0:CB], scale[0]),
                              (q4h[:], scale[1]))[k]
                    for x in range(2):
                        act.wait_ge(s_q[k][x], step)
                        a.activation(tanh_hl[:, CH * x:CH * (x + 1), 0:B], r8(src)[:, CH * x:CH * (x + 1)], ACT.Tanh,
                                     scale=s).then_inc(s_hi[k][x], 1)
                        a.activation(tanh_f[:, HALF * x:HALF * (x + 1)], src[:, HALF * x:HALF * (x + 1)], ACT.Tanh,
                                     scale=s).then_inc(s_tf[k][x], 1)
                    if k == 0:
                        act.wait_ge(s_clip, step)
                        a.activation(qsq[:], q0_3[:], ACT.Square, scale=scale[2]).then_inc(s_sq[0], 1)
                        a.activation(trace[:, bass.ds(t * CB, CB)], q0_3[:], ACT.Copy, scale=1.0 / 3.0)
                    else:
                        a.activation(qsq[:], src, ACT.Square, scale=s).then_inc(s_sq[k], 1)
            act.wait_ge(s_clip, T + 1)
            a.activation(trace[:, T * CB:(T + 1) * CB], q0_3[:], ACT.Copy, scale=1.0 / 3.0).then_inc(s_tr, 1)
            a.preload_act_table(ACT.Exp)

            def x2_first(f):
                S["xtr"].wait(act, f, 1)
                S["x3"].wait(act, f, 0)
                S["x2"].by(a.copy(x2[:, 0], bank[6][:]))

            def queries_values(f):
                S["proj"].wait(act, f, 1)
                S["st"].wait(act, f, 0)
                S["qkv2"].by(a.activation(q2t[0:DK, :], bank[6][0:DK, :], ACT.Copy, scale=SCALE2))
                S["proj"].wait(act, f, 2)
                S["pv"].wait(act, f, 0)
                S["qkv2"].by(a.copy(v2[:, :, 0:DK], bank[7][:, 0:C * DK].rearrange("p (c k) -> p c k", c=C)))

            def max_row(f):
                S["mt"].wait(act, f, 1)
                S["mrow"].by(a.copy(q2t[64:65, :], bank[6][0:1, :]))

            def key_exps(f, n):
                for kc in (2 * n, 2 * n + 1):
                    S["st"].wait(act, f, kc + 1)
                    S["e2"].by(a.activation(e2[:, kc], bank[6 + kc % 2][:], ACT.Exp))

            def head_turned(f):
                S["h2t"].wait(act, f, 1)
                S["h2e"].by(a.copy(head2t[:], bank[7][0:DK, :]))

            def x3_squares(f):
                S["xnp"].wait(act, f, 0)
                for tc in range(TC):
                    S["x3"].wait(act, f, tc + 1)
                    S["ss"].by(a.activation(x3n[:, tc], x3[:, tc], ACT.Square, accum_out=ss3[:, tc:tc + 1]))

            def normed_turned(f, b):
                S["par"].wait(act, f, 1)
                if b is not None:
                    S["qkv"].wait(act, b, 6)
                for dc in range(C):
                    if dc % 2 == 0:
                        S["xnp"].wait(act, f, dc // 2 + 1)
                    S["xnt"].by(a.activation(xnt[:, dc], bank[6 + dc // 2][:, (dc % 2) * T:(dc % 2 + 1) * T],
                                             ACT.Identity, bias=par[:, 8 + dc:9 + dc], scale=par[:, 4 + dc:5 + dc]))

            def back(b, f):
                def squares(i):
                    S["qkv"].wait(act, b, i + 1)
                    if i >= 2:
                        S["hs"].wait(act, b, i - 1)
                    S["sqr"].by(a.activation(sqs[i % 2][:], bank[i // 2 * 3 + i % 2][:], ACT.Square))

                def values(tc):
                    S["qkv"].wait(act, b, tc + 5)
                    S["pv3"].wait(act, b, 0)
                    S["v3"].by(a.activation(v3h[:, tc], bank[tc * 3 + 2][:], ACT.Copy, scale=vscale[:, 0:1]))

                squares(0)
                if f is not None:
                    x2_first(f)
                squares(1)
                squares(2)
                if f is not None:
                    queries_values(f)
                squares(3)

                def turned(i):
                    tc, j = i // 2, i % 2
                    S["qkp"].wait(act, b, i + 1)
                    for r in ((0, 1), (HPC,))[j]:
                        S["qkt"].by(a.activation((*qth, kt)[r][:, :, tc * P:(tc + 1) * P],
                                                 bank[tc * 3 + j][:].rearrange("p (c t) -> p c t", c=C), ACT.Copy,
                                                 scale=gains[:, r:r + 1]))

                turned(0)
                turned(1)
                values(0)
                turned(2)
                turned(3)
                values(1)

                def exps(h):
                    S["m3"].wait(act, b, h + 1)
                    if h >= 2:
                        S["et"].wait(act, b, h - 1)
                    for tc in range(TC):
                        e = a.activation(e3[h % 2][:, tc], bank[h % 2][:, tc * T:(tc + 1) * T], ACT.Exp,
                                         bias=negmax3[:, h % 2, tc:tc + 1],
                                         accum_out=den3[:, tc, h:h + 1])
                    S["e3"].by(e)

                exps(0)
                exps(1)
                for h in range(NH):
                    S["et"].wait(act, b, h + 1)
                    if h >= 2:
                        S["pv3"].wait(act, b, h - 1)
                        S["etl"].wait(act, b, h - 1)
                    S["eth"].by(a.copy(e3t_hi[h % 2][:].rearrange("p k t -> p (k t)"), bank[2 + h % 2][:]))
                    if h + 2 < NH:
                        exps(h + 2)
                    if f is not None:
                        if h == MAX_ROW:
                            max_row(f)
                        if h - 1 in KEY_SCORES:
                            key_exps(f, KEY_SCORES.index(h - 1))
                        if h == HEAD_TURNED:
                            head_turned(f)
                        if h == L2_OUT + 2:
                            x3_squares(f)
                        if h == NORMED:
                            normed_turned(f, b)
                for tc in range(TC):
                    S["ot"].wait(act, b, tc + 1)
                    S["ote"].by(a.copy(o_t[:, 2 * tc:2 * tc + 2], bank[2 + tc][:].rearrange("p (c t) -> p c t", c=2)))

            x2_first(0)
            queries_values(0)
            act.wait_ge(s_vs, 1)
            max_row(0)
            key_exps(0, 0)
            key_exps(0, 1)
            head_turned(0)
            x3_squares(0)
            normed_turned(0, None)
            with act.Fori(0, B - 1) as b:
                back(b, b + 1)
            back(B - 1, None)

        @block.tensor
        def _(pe):
            mm = nc.tensor.matmul
            tr = nc.tensor.transpose
            pe.wait_ge(s_id, 1)
            pe.wait_ge(s_lr, 16 * 9)
            for c in range(C):
                ins = tr(bank[4][:, c * 16:(c + 1) * 16], rows[:, c * P:(c + 1) * P], ident[0:16, 0:16])
            ins.then_inc(s_colp, 1)
            with pe.Fori(0, B // 2) as i:
                for j in range(4):
                    pe.wait_ge(s_xl[j], i * 16 + 16)
                    pe.wait_ge(s_xe[j % 2], i * 2 + (j // 2 + 1))
                    for c in range(C):
                        ins = tr(bank[j][:, c * P:(c + 1) * P], xl[j][:, c * P:(c + 1) * P], ident[:])
                    ins.then_inc(s_xt, 1)
            pe.wait_ge(s_lc, 16)
            for mc in range(C):
                pe.wait_ge(s_xe[mc % 2], B + 1)
                for n in range(C):
                    ins = tr(bank[mc][:, n * P:(n + 1) * P], coup[:, n, mc * P:(mc + 1) * P], ident[:])
                ins.then_inc(s_ct, 1)
            pe.wait_ge(s_chi, 2)
            with pe.Fori(0, T) as t:
                step = pe.snap(t + 1)
                for k in range(4):
                    def lows(x, y):
                        for kc in range(CH * x, CH * (x + 1)):
                            for m in range(CH):
                                mm(ps_prod[y][:, y, m * B:(m + 1) * B],
                                   c_lo[:, kc, (CH * y + m) * P:(CH * y + m + 1) * P], tanh_hl[:, kc, 0:B],
                                   start=(kc == 0 and m == 0), stop=False, skip_group_check=True)

                    def highs(x, y):
                        for m in range(CH):
                            for kc in range(CH * x, CH * (x + 1)):
                                both = tanh_hl[:, kc, :].rearrange("p (s b) -> p s b", s=2)
                                ins = mm(ps_prod[y][:, :, m * B:(m + 1) * B],
                                         c_hi[:, kc, (CH * y + m) * P:(CH * y + m + 1) * P], both,
                                         start=False, stop=(kc == C - 1 and m == CH - 1), skip_group_check=True)
                        return ins

                    pe.wait_ge(s_hi[k][0], step)
                    lows(0, 0)
                    pe.wait_ge(s_q[k][1], step)
                    lows(0, 1)
                    pe.wait_ge(s_hi[k][1], step)
                    lows(1, 0)
                    pe.wait_ge(s_lo[k][0], step)
                    highs(0, 0)
                    highs(0, 1)
                    pe.wait_ge(s_lo[k][1], step)
                    highs(1, 0).then_inc(s_mm[k][0], 1)
                    lows(1, 1)
                    highs(1, 1).then_inc(s_mm[k][1], 1)
            pe.wait_ge(s_q[0][1], T + 1)

            def x2_turns(f):
                S["xnt"].wait(pe, f, 0)
                S["x2t"].wait(pe, f, 4)
                for tc in range(TC):
                    for c in range(C):
                        ins = tr(bank[6 + tc][:, c * P:(c + 1) * P], x2t[:, c, tc * P:(tc + 1) * P], ident[:])
                    S["xtr"].by(ins)

            def projections(f):
                S["x2"].wait(pe, f, 2)
                for tc in range(TC):
                    ins = mm(bank[6][:], wqk2[:, tc], x2[:, tc], start=(tc == 0), stop=(tc == TC - 1))
                S["proj"].by(ins)
                for c in range(C):
                    for tc in range(TC):
                        ins = mm(bank[7][:, c * DK:(c + 1) * DK], x2[:, tc, c * P:(c + 1) * P], wv2[:, tc],
                                 start=(tc == 0), stop=(tc == TC - 1))
                S["proj"].by(ins)

            def query_scores(f, n):
                if n == 0:
                    S["qkv2"].wait(pe, f, 2)
                    S["kk"].wait(pe, f, 1)
                    S["hm_done"].wait(pe, f, 2)
                for qc in (2 * n, 2 * n + 1):
                    if qc >= 2:
                        S["mx"].wait(pe, f, qc - 1)
                    S["sc"].by(mm(bank[6 + qc % 2][:], q2t[0:64, qc * P:(qc + 1) * P], k2t[0:64, :], start=True,
                                  stop=True))

            def max_row(f):
                S["mx"].wait(pe, f, 4)
                for qc in range(C):
                    ins = tr(bank[6][0:1, qc * P:(qc + 1) * P], negmax2[:, qc:qc + 1], ident[:])
                S["mt"].by(ins)

            def key_scores(f, n):
                if n == 0:
                    S["mrow"].wait(pe, f, 1)
                for kc in (2 * n, 2 * n + 1):
                    if kc >= 2:
                        S["e2"].wait(pe, f, kc - 1)
                    S["st"].by(mm(bank[6 + kc % 2][:], k2t[0:65, kc * P:(kc + 1) * P], q2t[0:65, :], start=True,
                                  stop=True))

            def weighted_values(f, n):
                S["e2"].wait(pe, f, 4)
                for qc in (2 * n, 2 * n + 1):
                    for kc in range(C):
                        ins = mm(bank[6][:, qc * 17:(qc + 1) * 17], e2[:, kc, qc * P:(qc + 1) * P], v2[:, kc],
                                 start=(kc == 0), stop=(kc == C - 1))
                if n == 1:
                    S["pv"].by(ins)

            def head_turned(f):
                S["h2"].wait(pe, f, 3)
                for qc in range(C):
                    ins = tr(bank[7][0:DK, qc * P:(qc + 1) * P], head2[:, qc], ident[:])
                S["h2t"].by(ins)

            def l2_out(f):
                S["h2e"].wait(pe, f, 1)
                for tc in range(TC):
                    S["o2"].by(mm(bank[6 + tc][:], wo_sum[:, tc * P:(tc + 1) * P], head2t[:], start=True, stop=True))

            def normed_turns(f):
                for dc in range(C):
                    for tc in range(TC):
                        S["x3n"].wait(pe, f, tc + 1)
                        ins = tr(bank[6 + dc // 2][:, (dc % 2) * T + tc * P:(dc % 2) * T + (tc + 1) * P],
                                 x3n[:, tc, dc * P:(dc + 1) * P], ident[:])
                    if dc % 2:
                        S["xnp"].by(ins)

            def qkv(b, m):
                if m == 0:
                    S["xnt"].wait(pe, b, 4)
                tc, j = m // 3, m % 3
                for dc in range(C):
                    ins = mm(bank[m][:], xnt[:, dc, tc * P:(tc + 1) * P], wqkv[:, dc, j * D:(j + 1) * D],
                             start=(dc == 0), stop=(dc == C - 1))
                S["qkv"].by(ins)

            def back(b, f):
                def qk_turns(i):
                    S["qkn"].wait(pe, b, i + 1)
                    for c in range(C):
                        ins = tr(bank[i // 2 * 3 + i % 2][:, c * P:(c + 1) * P], qkn[i % 2][:, c * P:(c + 1) * P],
                                 ident[:])
                    S["qkp"].by(ins)

                if f is not None:
                    x2_turns(f)
                S["ote"].wait(pe, b, 0)
                qkv(b, 3)
                if f is not None:
                    projections(f)
                S["res"].wait(pe, b, 0)
                qkv(b, 4)
                if f is not None:
                    query_scores(f, 0)
                qkv(b, 2)
                qk_turns(0)
                qk_turns(1)
                qkv(b, 5)
                qk_turns(2)
                qk_turns(3)
                if f is not None:
                    query_scores(f, 1)
                S["qkt"].wait(pe, b, 6)
                S["qkt2"].wait(pe, b, 4)

                def scores(h):
                    c = h // HPC
                    if h >= 2:
                        S["e3"].wait(pe, b, h - 1)
                    for tc in range(TC):
                        ins = mm(bank[h % 2][:, tc * T:(tc + 1) * T], qth[h % HPC][:, c, tc * P:(tc + 1) * P],
                                 kt[:, c, :], start=True, stop=True)
                    S["s3"].by(ins)

                def turn(h):
                    S["e3"].wait(pe, b, h + 1)
                    if h >= 2:
                        S["etl"].wait(pe, b, h - 1)
                        S["eth"].wait(pe, b, h - 1)
                    for kc in range(TC):
                        for tc in range(TC):
                            ins = tr(bank[2 + h % 2][:, kc * T + tc * P:kc * T + (tc + 1) * P],
                                     e3[h % 2][:, tc, kc * P:(kc + 1) * P], ident[:])
                    S["et"].by(ins)

                def pv(h):
                    S["etl"].wait(pe, b, h + 1)
                    for tc in range(TC):
                        for n, (kc, e, vv) in enumerate((kc, e, vv) for e, vv in
                                                        ((e3t_lo, v3h), (e3t_hi, v3l), (e3t_hi, v3h))
                                                        for kc in range(TC)):
                            ins = mm(bank[4 + tc][:, h * DH:(h + 1) * DH], e[h % 2][:, kc, tc * P:(tc + 1) * P],
                                     vv[:, kc, h * DH:(h + 1) * DH], start=(n == 0), stop=(n == 3 * TC - 1))
                    S["pv3"].by(ins)

                scores(0)
                scores(1)
                S["v3l"].wait(pe, b, 2)
                for h in range(NH):
                    if h + 2 < NH:
                        scores(h + 2)
                    if h >= 2:
                        pv(h - 2)
                    turn(h)
                    if f is not None:
                        if h == MAX_ROW:
                            max_row(f)
                        if h in KEY_SCORES:
                            key_scores(f, KEY_SCORES.index(h))
                        if h in WEIGHTED:
                            weighted_values(f, WEIGHTED.index(h))
                        if h == HEAD_TURNED:
                            head_turned(f)
                        if h == L2_OUT:
                            l2_out(f)
                        if h == NORMED:
                            normed_turns(f)
                pv(NH - 2)
                if f is not None:
                    qkv(f, 0)
                pv(NH - 1)
                if f is not None:
                    qkv(f, 1)
                for dc in range(C):
                    for tc in range(TC):
                        S["on"].wait(pe, b, tc + 1)
                        ins = tr(bank[2 + dc // 2][:, (dc % 2) * T + tc * P:(dc % 2) * T + (tc + 1) * P],
                                 o_sb[:, tc, dc * P:(dc + 1) * P], ident[:])
                    if dc % 2:
                        S["ot"].by(ins)
                S["ote"].wait(pe, b, 2)
                for tc in range(TC):
                    for dc in range(C):
                        ins = mm(bank[4 + tc][:], o_t[:, dc, tc * P:(tc + 1) * P], wout[:, dc], start=(dc == 0),
                                 stop=(dc == C - 1))
                    S["op"].by(ins)

            x2_turns(0)
            projections(0)
            pe.wait_ge(s_ld, 16 * 7)
            pe.wait_ge(s_cols, 1)
            for n in range(2 * C):
                for c in range(C):
                    ins = mm(bank[4][:, 64 + n * B:64 + (n + 1) * B], wemb[:, c, n * P:(n + 1) * P], cols[:, c, 0:B],
                             start=(c == 0), stop=(c == C - 1))
            ins.then_inc(s_emb, 1)
            pe.wait_ge(s_fold, 1)
            for c in range(2):
                ins = mm(bank[5][0:DK, 0:T], fold[:], wo2[:, c], start=(c == 0), stop=(c == 1))
            ins.then_inc(s_wos, 1)
            query_scores(0, 0)
            query_scores(0, 1)
            max_row(0)
            key_scores(0, 0)
            key_scores(0, 1)
            weighted_values(0, 0)
            weighted_values(0, 1)
            head_turned(0)
            l2_out(0)
            normed_turns(0)
            qkv(0, 0)
            qkv(0, 1)
            with pe.Fori(0, B - 1) as b:
                back(b, b + 1)
            back(B - 1, None)

        @block.vector
        def _(dve):
            v = nc.vector
            STT = v.scalar_tensor_tensor
            chain = [0]

            def link(ins):
                chain[0] += 1
                ins.then_inc(s_vec0, 1)
                dve.wait_ge(s_vec0, chain[0])

            dve.wait_ge(s_lc, 16)
            v.tensor_reduce(cmax[:, 0:1], coup.rearrange("p c m -> p (c m)"), AX.X, ALU.max,
                            apply_absolute_value=True).then_inc(s_cm, 1)
            dve.wait_ge(s_colp, 1)
            v.tensor_copy(cols[:].rearrange("p c r -> p (c r)"), bank[4][:, 0:64]).then_inc(s_cols, 1)
            dve.wait_ge(s_cols, 1)
            dve.wait_ge(s_cma, 1)
            link(v.tensor_scalar(pow2[:, 0:1], cmax[:, 1:2], H, 2.0 ** -40, ALU.mult, ALU.max))
            link(v.tensor_scalar(pow2[:, 0:1], pow2[:, 0:1], 2.0 ** 60, None, ALU.min))
            link(v.tensor_scalar(ebits[:, 0:1], pow2[:, 0:1].bitcast(I32), 0x7F800000, None, ALU.bitwise_and))
            link(v.tensor_scalar(ebits[:, 1:2], ebits[:, 0:1], -1.0, float(254 << 23), ALU.mult, ALU.add))
            two_e, two_me = ebits[:, 0:1].bitcast(F32), ebits[:, 1:2].bitcast(F32)
            for n, (src, f) in enumerate(((two_e, 2.0 ** -14), (two_e, 2.0 ** -13), (two_e, 2.0 ** -14 / 3),
                                          (two_me, H * 2.0 ** 14), (two_me, CLAMP * 2.0 ** 14),
                                          (two_me, -CLAMP * 2.0 ** 14), (two_me, (CLAMP - SHIFT) * 2.0 ** 14),
                                          (two_me, (-CLAMP - SHIFT) * 2.0 ** 14), (two_me, -SHIFT * 2.0 ** 14),
                                          (two_e, 2.0 ** -14 / H))):
                v.tensor_scalar(cs[:, n:n + 1], src, f, None, ALU.mult)
            link(v.tensor_scalar(pow2[:, 1:2], two_me, 2.0 ** 14, None, ALU.mult))
            v.tensor_copy(taps[:].rearrange("p k (c b) -> p k c b", b=B),
                          cols[:, :, 0:TAPS].rearrange("p c k -> p k c").unsqueeze(3).to_broadcast([P, TAPS, C, B]))
            link(v.tensor_scalar(neg_bias[:], cols[:, :, 9], -1.0, SHIFT, ALU.mult, ALU.add))
            link(v.tensor_tensor(bias_diff[:], cols[:, :, 8], neg_bias[:], ALU.subtract))
            v.tensor_copy(r8(conv_bias[:]), bias_diff[:].unsqueeze(2).to_broadcast([P, C, B]))
            v.tensor_copy(h_sigma[:], cs[:, 3:4].to_broadcast([P, CB])).then_inc(s_par, 1)
            v.memset(q_upper[:], BIG)
            v.memset(q_lower[:], -BIG)
            v.memset(p_upper[:], BIG)
            v.memset(p_lower[:], -BIG)
            link(v.tensor_scalar(r8(Z[0][:, 0:CB]), cols[:, :, 0:B], pow2[:, 1:2], None, ALU.mult))
            v.tensor_scalar(q3, Z[0][:, 0:CB], 3.0, None, ALU.mult)
            link(v.tensor_scalar(p3, Z[0][:, 0:CB], cs[:, 8:9], None, ALU.add))
            link(v.tensor_scalar(p3, p3, 3.0, None, ALU.mult))
            link(v.tensor_reduce(of_head[:], ident[:].rearrange("p (r j) -> p r j", j=DH), AX.X, ALU.add))
            link(v.tensor_scalar(gains[:, HPC:HPC + 1], cols[:, 0, 14:15], SCALE3, None, ALU.mult))
            link(v.tensor_scalar(gains[:, 0:HPC], of_head[:], cols[:, 0, 13:14], None, ALU.mult))
            v.tensor_reduce(fold[:], ident[:].rearrange("p (a j) -> p j a", j=DK), AX.X, ALU.add).then_inc(s_fold, 1)
            with dve.Fori(0, B // 2) as i:
                for j in (0, 2):
                    dve.wait_ge(s_xt, i * 4 + (j + 5))
                    bb, tc = i * 2 + j // 2, j % 2
                    dst = padded[:, (TAPS - 1 + tc * P) * CB:(TAPS - 1 + (tc + 1) * P) * CB] \
                        .rearrange("p (t c b) -> p b c t", c=C, b=B)
                    v.tensor_copy(dst[:, bass.ds(bb, 1)].rearrange("p o c t -> p (o c) t"),
                                  bank[j][:].rearrange("p (c t) -> p c t", c=C)).then_inc(s_xe[0], 1)
            for mc in range(C):
                dve.wait_ge(s_hic, mc + 1)
                ins = STT(c_lo[:, mc], bank[mc][:], cs[:, 3:4], c_hi[:, mc], ALU.mult, ALU.subtract)
            ins.then_inc(s_chi, 1)
            v.tensor_scalar(q3, Z[0][:, 0:CB], 3.0, None, ALU.mult).then_inc(s_chi, 1)
            v.tensor_scalar(cs[:, 9:10], two_e, 2.0 ** -14 / H, None, ALU.mult).then_inc(s_const, 1)
            dve.wait_ge(s_chi, 2)
            dve.wait_ge(s_const, 1)
            for x in range(2):
                v.tensor_copy(yv[:, x:x + 1], q3[:, x:x + 1]).then_inc(s_q[0][x], 1)

            FIRST = 1

            def reduced(k, x, step):
                if x == 0:
                    dve.wait_ge(s_b[k], step)
                dve.wait_ge(s_mm[k][x], step)
                v.tensor_reduce((Z[1], Z[2], q4h, sum3)[k][:, HALF * x:HALF * (x + 1)],
                                ps_half[x].rearrange("p s c -> p c s"), AX.X,
                                ALU.add).then_inc(s_q[(k + 1) % 4][x], 1)

            def clip_q(step):
                dve.wait_ge(s_q[0][0], step)
                dve.wait_ge(s_q[0][1], step)
                STT(q0_3[:], q3, q_upper[:], q_lower[:], ALU.min, ALU.max).then_inc(s_clip, 1)

            def p_below(step):
                dve.wait_ge(s_up, step)
                v.tensor_tensor(Z[0][:, CB:2 * CB], p_up[:], p_lower[:], ALU.max).then_inc(s_p0, 1)

            def p_above():
                STT(p_up[:], p3, 1.0 / 3.0, p_upper[:], ALU.mult, ALU.min).then_inc(s_up, 1)

            def low_part(k, x, step):
                dve.wait_ge(s_tf[k][x], step)
                c = slice(CH * x, CH * (x + 1))
                v.tensor_tensor(tanh_hl[:, c, B:2 * B], r8(tanh_f[:])[:, c], tanh_hl[:, c, 0:B],
                                ALU.subtract).then_inc(s_lo[k][x], 1)

            def addend(k, step, dr):
                q, p = Z[k][:, 0:CB], Z[k][:, CB:2 * CB]
                if k == 0:
                    p_below(step)
                    clip_q(step)
                    low_part(0, 0, step)
                    dve.wait_ge(s_clip, step)
                    dve.wait_ge(s_drv, step)
                    STT(q_hd[:], q0_3[:], 1.0 / 3.0, dr, ALU.mult, ALU.add).then_inc(s_hd[0], 1)
                    low_part(0, 1, step)
                if k == 1:
                    dve.wait_ge(s_p[1], step)
                    v.tensor_tensor(acc[:, CB:2 * CB], Z[1][:, CB:2 * CB], Z[0][:, CB:2 * CB], ALU.subtract)
                if k in (1, 2):
                    dve.wait_ge(s_q[k][0], step)
                    dve.wait_ge(s_q[k][1], step)
                    STT(yv[:], p, -BETA, q, ALU.mult, ALU.add).then_inc(s_y[k], 1)
                    low_part(k, 0, step)
                    if k == 1:
                        STT(acc[:, 0:CB], q0_3[:], -1.0 / 3.0, q, ALU.mult, ALU.add).then_inc(s_acc[1], 1)
                    else:
                        dve.wait_ge(s_acc[1], step)
                        STT(acc[:], Z[2][:], 2.0, acc[:], ALU.mult, ALU.add).then_inc(s_acc[2], 1)
                    low_part(k, 1, step)
                if k == 3:
                    dve.wait_ge(s_q[3][0], step)
                    dve.wait_ge(s_q[3][1], step)
                    dve.wait_ge(s_accd, step)
                    STT(acc_hd[:], q4h[:], 2.0, acc_d[:], ALU.mult, ALU.add).then_inc(s_hd[3], 1)
                    low_part(3, 0, step)
                    STT(acc[:, CB:2 * CB], p, 1.0 - H * EPSILON * BETA, acc[:, CB:2 * CB], ALU.mult,
                        ALU.add).then_inc(s_accp, 1)
                    low_part(3, 1, step)
                dve.wait_ge(s_sq[k], step)
                STT(cub[:], qsq[:], 3.0, (q0_3[:], q, q, q4h[:])[k], ALU.subtract, ALU.mult)
                if k in (0, 3):
                    dve.wait_ge(s_hd[k], step)
                if k == 0:
                    dve.wait_ge(s_p0, step)
                if k == 2:
                    dve.wait_ge(s_hd2, step)
                STT(wv_[:], p, -H, (q_hd, q_hd, q_hd2, acc_hd)[k][:], ALU.mult, ALU.add).then_inc(s_w[k], 1)
                if k == 0:
                    v.tensor_scalar(p_kept[:], p, 1.0 - H * EPSILON * BETA, None, ALU.mult).then_inc(s_y[0], 1)
                if k in (1, 2):
                    dve.wait_ge(s_y[k], step)
                    STT(Z[k + 1][:, CB:2 * CB], yv[:], (1, 1, 2)[k] * H * EPSILON, Z[0][:, CB:2 * CB],
                        ALU.mult, ALU.add).then_inc(s_p[k + 1], 1)
                if k == 3:
                    dve.wait_ge(s_accp, step)
                    STT(p3, q4h[:], 2 * H * EPSILON, acc[:, CB:2 * CB], ALU.mult, ALU.add).then_inc(s_p3, 1)
                dve.wait_ge(s_w[k], step)
                STT(psC[:, 2:4, 0:HALF], cub[:].rearrange("p (x c) -> p x c", x=2), -(1 / 3, 1, 1, 2)[k] * H / 3,
                    wv_[:].rearrange("p (x c) -> p x c", x=2), ALU.mult, ALU.add).then_inc(s_b[k], 1)
                if k == 0:
                    dve.wait_ge(s_y[0], step)
                    STT(Z[1][:, CB:2 * CB], q0_3[:], H * EPSILON / 3, p_kept[:], ALU.mult,
                        ALU.add).then_inc(s_p[1], 1)
                if k == 3:
                    if step is FIRST:
                        link(v.tensor_copy(p_upper[:], cs[:, 6:7].to_broadcast([P, CB])))
                        link(v.tensor_copy(p_lower[:], cs[:, 7:8].to_broadcast([P, CB])))
                    dve.wait_ge(s_p3, step)
                    p_above()

            def stages(step, dr):
                for k in range(3):
                    addend(k, step, dr)
                    reduced(k, 0, step)
                    if k == 0:
                        STT(q_hd2[:], q0_3[:], 1.0 / 6.0, dr, ALU.mult, ALU.add).then_inc(s_hd2, 1)
                    if k == 2:
                        dve.wait_ge(s_acc[2], step)
                        v.tensor_tensor(acc_d[:], dr, acc[:, 0:CB], ALU.add).then_inc(s_accd, 1)
                    reduced(k, 1, step)
                addend(3, step, dr)

            p_above()
            stages(FIRST, drive[:, 0])
            v.tensor_scalar(q_upper[:], cs[:, 4:5], 3.0, None, ALU.mult)
            link(v.tensor_scalar(q_lower[:], cs[:, 5:6].to_broadcast([P, CB]), 3.0, None, ALU.mult))
            STEPS = 5
            assert (T - 1) % STEPS == 0
            drives = drive[:].rearrange("p t c -> p (t c)")
            with dve.Fori(0, (T - 1) // STEPS) as turn:
                step = dve.snap(turn * STEPS + 1)
                for i in range(STEPS):
                    after = dve.snap(turn * STEPS + (i + 2))
                    at = dve.snap(turn * (STEPS * CB) + (i + 1) * CB)
                    reduced(3, 0, step)
                    reduced(3, 1, step)
                    step = after
                    stages(step, drives[:, bass.ds(at, CB)])
            reduced(3, 0, T)
            reduced(3, 1, T)
            clip_q(T + 1)
            def x2_second(f):
                S["xtr"].wait(dve, f, 2)
                S["x2"].by(v.tensor_copy(x2[:, 1], bank[7][:]))

            def keys(f):
                S["proj"].wait(dve, f, 1)
                S["qkv2"].wait(dve, f, 1)
                S["hm"].wait(dve, f, 32)
                S["kk"].by(v.tensor_tensor(k2t[0:DK, :], bank[6][32:32 + DK, :], hmask[:], ALU.mult))

            def query_maxima(f, n):
                for qc in (2 * n, 2 * n + 1):
                    S["sc"].wait(dve, f, qc + 1)
                    S["mx"].by(v.tensor_reduce(negmax2[:, qc:qc + 1], bank[6 + qc % 2][:], AX.X, ALU.max, negate=True))

            def head(f):
                S["pv"].wait(dve, f, 1)
                O = bank[6][:, 0:C * 17].rearrange("p (c k) -> p c k", k=17)
                S["h2"].by(v.reciprocal(rden2[:], O[:, :, DK]))
                S["par"].wait(dve, f, 1)
                S["h2"].wait(dve, f, 1)
                S["h2"].by(v.tensor_tensor(rmask2[:], rden2[:], par[:, 0:C], ALU.mult))
                S["h2"].wait(dve, f, 2)
                S["h2"].by(v.tensor_tensor(head2[:], O[:, :, 0:DK], rmask2[:].unsqueeze(2).to_broadcast([P, C, DK]),
                                           ALU.mult))

            def x3_sum(f):
                S["keep"].wait(dve, f, 0)
                for tc in range(TC):
                    S["o2"].wait(dve, f, tc + 1)
                    S["x3"].by(v.tensor_tensor(x3[:, tc], bank[6 + tc][:], x2[:, tc], ALU.add))

            def x3_mean(f):
                S["ss"].wait(dve, f, 2)
                S["ms"].by(v.tensor_scalar(ms3[:], ss3[:], 1.0 / D, RMS_EPS, ALU.mult, ALU.add))

            def x3_normed(f):
                S["r3"].wait(dve, f, 1)
                S["xnp"].wait(dve, f, 0)
                for tc in range(TC):
                    S["x3n"].by(v.tensor_scalar(x3n[:, tc], x3[:, tc], r3[:, tc:tc + 1], None, ALU.mult))

            def back(b, f):
                def head_queries(tc):
                    S["qkt"].wait(dve, b, 3 * tc + 2)
                    for r in (2, 3):
                        S["qkt2"].by(v.tensor_scalar(qth[r][:, :, tc * P:(tc + 1) * P],
                                                     bank[tc * 3][:].rearrange("p (c t) -> p c t", c=C),
                                                     gains[:, r:r + 1], None, ALU.mult))

                def sums(i):
                    S["sqr"].wait(dve, b, i + 1)
                    S["hs"].by(v.tensor_reduce(hss[:, i], sqs[i % 2][:].rearrange("p (h d) -> p h d", d=DH), AX.X,
                                               ALU.add))
                    S["hs"].wait(dve, b, i + 1)
                    S["hm3"].by(v.tensor_scalar(hms[:, i], hss[:, i], 1.0 / DH, RMS_EPS, ALU.mult, ALU.add))

                def normed(i):
                    S["hr"].wait(dve, b, i + 1)
                    if i >= 2:
                        S["qkp"].wait(dve, b, i - 1)
                    S["qkn"].by(v.tensor_tensor(qkn[i % 2][:].rearrange("p (h d) -> p h d", d=DH),
                                                bank[i // 2 * 3 + i % 2][:].rearrange("p (h d) -> p h d", d=DH),
                                                hr[:, i].unsqueeze(2).to_broadcast([P, NH, DH]), ALU.mult))

                def values_low(tc):
                    S["v3"].wait(dve, b, tc + 1)
                    S["v3l"].by(STT(v3l[:, tc], bank[tc * 3 + 2][:], vscale[:, 0:1], v3h[:, tc], ALU.mult,
                                    ALU.subtract))

                sums(0)
                if f is not None:
                    x2_second(f)
                sums(1)
                normed(0)
                normed(1)
                sums(2)
                if f is not None:
                    keys(f)
                sums(3)
                normed(2)
                normed(3)
                if f is not None:
                    query_maxima(f, 0)
                head_queries(0)
                values_low(0)
                head_queries(1)
                values_low(1)
                if f is not None:
                    query_maxima(f, 1)

                def maxima(h):
                    S["s3"].wait(dve, b, h + 1)
                    S["m3"].by(v.tensor_reduce(negmax3[:, h % 2], bank[h % 2][:].rearrange("p (q k) -> p q k", k=T),
                                               AX.X, ALU.max, negate=True))

                maxima(0)
                maxima(1)
                for h in range(NH):
                    if h + 2 < NH:
                        maxima(h + 2)
                    S["eth"].wait(dve, b, h + 1)
                    if h >= 2:
                        S["pv3"].wait(dve, b, h - 1)
                    S["etl"].by(v.tensor_tensor(e3t_lo[h % 2][:].rearrange("p k t -> p (k t)"), bank[2 + h % 2][:],
                                                e3t_hi[h % 2][:].rearrange("p k t -> p (k t)"), ALU.subtract))
                    if f is not None:
                        if h == WEIGHTED[1] + 1:
                            head(f)
                        if h == L2_OUT + 1:
                            x3_sum(f)
                        if h == L2_OUT + 3:
                            x3_mean(f)
                        if h == L2_OUT + 4:
                            x3_normed(f)
                S["e3"].wait(dve, b, NH)
                S["rd"].by(v.tensor_scalar(den3[:], den3[:], vscale[:, 0:1], None, ALU.mult))
                S["rd"].wait(dve, b, 1)
                S["rd"].by(v.reciprocal(rden3[:], den3[:]))
                S["rd"].wait(dve, b, 2)
                S["pv3"].wait(dve, b, NH)
                for tc in range(TC):
                    S["on"].by(v.tensor_tensor(o_sb[:, tc].rearrange("p (h d) -> p h d", d=DH),
                                               bank[4 + tc][:].rearrange("p (h d) -> p h d", d=DH),
                                               rden3[:, tc].unsqueeze(2).to_broadcast([P, NH, DH]), ALU.mult))
                S["on"].wait(dve, b, 2)
                S["stored"].wait(dve, b, 0)
                S["keep"].wait(dve, b, 1)
                for tc in range(TC):
                    S["rs"].by(v.tensor_tensor(res[:, tc], o_sb[:, tc], x3k[:, tc], ALU.add))
                for tc in range(TC):
                    S["rs"].wait(dve, b, tc + 1)
                    S["op"].wait(dve, b, tc + 1)
                    S["res"].by(v.tensor_tensor(res[:, tc], bank[4 + tc][:], res[:, tc], ALU.add))

            x2_second(0)
            keys(0)
            dve.wait_ge(s_emb, 1)
            emb = bank[4][:, 64:64 + 2 * CB].rearrange("p (n b) -> p n b", b=B)
            pr = params[:].rearrange("p b n -> p n b")
            v.tensor_copy(pr[:, 0:4], cols[:, :, 0:B])
            bc = lambda r: cols[:, :, r:r + 1].to_broadcast([P, C, B])
            v.tensor_tensor(pr[:, 8:12], emb[:, 4:8], bc(12), ALU.add)
            link(v.tensor_tensor(pr[:, 4:8], emb[:, 0:4], bc(11), ALU.add))
            link(v.tensor_scalar(pr[:, 4:8], pr[:, 4:8], 1.0, None, ALU.add))
            v.tensor_tensor(pr[:, 4:8], pr[:, 4:8], bc(10), ALU.mult).then_inc(s_prm, 1)
            dve.wait_ge(s_prm, 1)
            dve.wait_ge(s_ld, 16 * 7)
            v.tensor_reduce(vmax[:, 0:1], params[:, :, 4:12], AX.XY, ALU.max,
                            apply_absolute_value=True)
            link(v.tensor_reduce(wvmax[:], wqkv[:, :, 2 * D:3 * D], AX.X, ALU.max, apply_absolute_value=True))
            v.tensor_reduce(vmax[:, 1:2], wvmax[:], AX.X, ALU.max).then_inc(s_vm, 1)
            dve.wait_ge(s_wos, 1)
            link(v.tensor_copy(wo_sum[:], bank[5][0:DK, 0:T]))
            dve.wait_ge(s_vma, 2)
            link(v.tensor_scalar(vscale[:, 1:2], vmax[:, 2:3], (D ** 0.5 + 1) * 1.01 * D, vmax[:, 3:4], ALU.mult,
                                 ALU.mult))
            link(v.tensor_scalar(vscale[:, 1:2], vscale[:, 1:2], 2.0 ** -100, 2.0 ** 100, ALU.max, ALU.min))
            link(v.tensor_scalar(vbits[:, 0:1], vscale[:, 1:2].bitcast(I32), 0x7F800000, None, ALU.bitwise_and))
            link(v.tensor_scalar(vbits[:, 1:2], vbits[:, 0:1], -1.0, float(254 << 23), ALU.mult, ALU.add))
            v.tensor_scalar(vscale[:, 0:1], vbits[:, 1:2].bitcast(F32), 2.0 ** 14, None,
                            ALU.mult).then_inc(s_vs, 1)
            dve.wait_ge(s_vs, 1)
            query_maxima(0, 0)
            query_maxima(0, 1)
            head(0)
            x3_sum(0)
            x3_mean(0)
            x3_normed(0)
            with dve.Fori(0, B - 1) as b:
                back(b, b + 1)
            back(B - 1, None)

        for name, signal_ in S.items():
            assert name in ("hm", "stored") or signal_.n == 2 * signal_.per, name


_INS = ["x", "cond_2048", "L0_cond_b", "L1_cond_coupling", "L1_cond_bias", "L2_cond_Wq", "L2_cond_Wk", "L2_cond_Wv",
        "L2_cond_Wo", "L3_cond_W_emb", "L3_cond_b_emb", "L3_cond_g_norm", "L3_cond_W_qkv", "L3_cond_g_q",
        "L3_cond_g_k", "L3_cond_W_out"]


def kernel(**inputs):
    import numpy as np
    import concourse.bacc as bacc
    from concourse import mybir
    from concourse.bass_utils import run_bass_kernel_spmd

    nc = bacc.Bacc("TRN2", target_bir_lowering=False, num_devices=1)
    arrays, args = {}, []
    for name in _INS:
        a = np.ascontiguousarray(inputs[name])
        arrays[f"in_{name}"] = a
        args.append(nc.dram_tensor(f"in_{name}", a.shape, mybir.dt.from_np(a.dtype), kind="ExternalInput").ap())
    args.append(nc.dram_tensor("out", inputs["x"].shape, mybir.dt.float32, kind="ExternalOutput").ap())
    build(nc, *args)
    r = run_bass_kernel_spmd(nc, [arrays], core_ids=[0])
    return r.results[0]["out"]
```
